# Optimizing a Trainium2 kernel written in Bass

```python
import numpy as np
import jax
import jax.numpy as jnp

def _softmax(x, axis=-1):
    return jax.nn.softmax(x, axis=axis)

def _gelu(x):
    return jax.nn.gelu(x, approximate=True)

def _silu(x):
    return jax.nn.silu(x)

def _sigmoid(x):
    return jax.nn.sigmoid(x)

def _layernorm(x, axis=-1, eps=1e-05):
    m = jnp.mean(x, axis=axis, keepdims=True)
    v = jnp.var(x, axis=axis, keepdims=True)
    return (x - m) / jnp.sqrt(v + eps)

def _scatter_add(tgt, idx, src, axis=0):
    return tgt.at[idx].add(src)

def _segment_sum(src, seg, n):
    return jax.ops.segment_sum(src, seg, n)
kernel_name = 'mk_dlrm_tower_d1_rec_r8_7d7c2f'

def setup_inputs(seed: int=0):
    np.random.seed(seed)
    _w = jnp.asarray

    def _rec_inputs():
        import jax
        import jax.numpy as jnp
        _tk = jax.random.key(seed)
        dense_ctx = jax.random.normal(jax.random.fold_in(_tk, 190), (512, 16), jnp.float32)
        ids = jnp.stack([jax.random.randint(jax.random.fold_in(_tk, 200 + f), (512,), 0, v, jnp.int32) for f, v in enumerate([1000, 125000, 125000, 1000, 1000, 125000, 1250, 12500, 1000, 1000, 12500, 12500, 12500, 12500, 1250, 1250, 1000, 12500, 12500, 1250, 1000, 12500, 1250, 1000, 1000, 1250, 1000, 1000, 1000, 1000, 1000, 1000, 1000, 1250, 1000, 1000, 1250, 1000, 1000, 1000])], axis=1)
        tbl_0 = 0.05 * jax.random.normal(jax.random.fold_in(_tk, 500 + 0), (1000, 64), jnp.float32)
        tbl_1 = 0.05 * jax.random.normal(jax.random.fold_in(_tk, 500 + 1), (125000, 64), jnp.float32)
        tbl_2 = 0.05 * jax.random.normal(jax.random.fold_in(_tk, 500 + 2), (125000, 64), jnp.float32)
        tbl_3 = 0.05 * jax.random.normal(jax.random.fold_in(_tk, 500 + 3), (1000, 64), jnp.float32)
        tbl_4 = 0.05 * jax.random.normal(jax.random.fold_in(_tk, 500 + 4), (1000, 64), jnp.float32)
        tbl_5 = 0.05 * jax.random.normal(jax.random.fold_in(_tk, 500 + 5), (125000, 64), jnp.float32)
        tbl_6 = 0.05 * jax.random.normal(jax.random.fold_in(_tk, 500 + 6), (1250, 64), jnp.float32)
        tbl_7 = 0.05 * jax.random.normal(jax.random.fold_in(_tk, 500 + 7), (12500, 64), jnp.float32)
        tbl_8 = 0.05 * jax.random.normal(jax.random.fold_in(_tk, 500 + 8), (1000, 64), jnp.float32)
        tbl_9 = 0.05 * jax.random.normal(jax.random.fold_in(_tk, 500 + 9), (1000, 64), jnp.float32)
        tbl_10 = 0.05 * jax.random.normal(jax.random.fold_in(_tk, 500 + 10), (12500, 64), jnp.float32)
        tbl_11 = 0.05 * jax.random.normal(jax.random.fold_in(_tk, 500 + 11), (12500, 64), jnp.float32)
        tbl_12 = 0.05 * jax.random.normal(jax.random.fold_in(_tk, 500 + 12), (12500, 64), jnp.float32)
        tbl_13 = 0.05 * jax.random.normal(jax.random.fold_in(_tk, 500 + 13), (12500, 64), jnp.float32)
        tbl_14 = 0.05 * jax.random.normal(jax.random.fold_in(_tk, 500 + 14), (1250, 64), jnp.float32)
        tbl_15 = 0.05 * jax.random.normal(jax.random.fold_in(_tk, 500 + 15), (1250, 64), jnp.float32)
        tbl_16 = 0.05 * jax.random.normal(jax.random.fold_in(_tk, 500 + 16), (1000, 64), jnp.float32)
        tbl_17 = 0.05 * jax.random.normal(jax.random.fold_in(_tk, 500 + 17), (12500, 64), jnp.float32)
        tbl_18 = 0.05 * jax.random.normal(jax.random.fold_in(_tk, 500 + 18), (12500, 64), jnp.float32)
        tbl_19 = 0.05 * jax.random.normal(jax.random.fold_in(_tk, 500 + 19), (1250, 64), jnp.float32)
        tbl_20 = 0.05 * jax.random.normal(jax.random.fold_in(_tk, 500 + 20), (1000, 64), jnp.float32)
        tbl_21 = 0.05 * jax.random.normal(jax.random.fold_in(_tk, 500 + 21), (12500, 64), jnp.float32)
        tbl_22 = 0.05 * jax.random.normal(jax.random.fold_in(_tk, 500 + 22), (1250, 64), jnp.float32)
        tbl_23 = 0.05 * jax.random.normal(jax.random.fold_in(_tk, 500 + 23), (1000, 64), jnp.float32)
        tbl_24 = 0.05 * jax.random.normal(jax.random.fold_in(_tk, 500 + 24), (1000, 64), jnp.float32)
        tbl_25 = 0.05 * jax.random.normal(jax.random.fold_in(_tk, 500 + 25), (1250, 64), jnp.float32)
        tbl_26 = 0.05 * jax.random.normal(jax.random.fold_in(_tk, 500 + 26), (1000, 64), jnp.float32)
        tbl_27 = 0.05 * jax.random.normal(jax.random.fold_in(_tk, 500 + 27), (1000, 64), jnp.float32)
        tbl_28 = 0.05 * jax.random.normal(jax.random.fold_in(_tk, 500 + 28), (1000, 64), jnp.float32)
        tbl_29 = 0.05 * jax.random.normal(jax.random.fold_in(_tk, 500 + 29), (1000, 64), jnp.float32)
        tbl_30 = 0.05 * jax.random.normal(jax.random.fold_in(_tk, 500 + 30), (1000, 64), jnp.float32)
        tbl_31 = 0.05 * jax.random.normal(jax.random.fold_in(_tk, 500 + 31), (1000, 64), jnp.float32)
        tbl_32 = 0.05 * jax.random.normal(jax.random.fold_in(_tk, 500 + 32), (1000, 64), jnp.float32)
        tbl_33 = 0.05 * jax.random.normal(jax.random.fold_in(_tk, 500 + 33), (1250, 64), jnp.float32)
        tbl_34 = 0.05 * jax.random.normal(jax.random.fold_in(_tk, 500 + 34), (1000, 64), jnp.float32)
        tbl_35 = 0.05 * jax.random.normal(jax.random.fold_in(_tk, 500 + 35), (1000, 64), jnp.float32)
        tbl_36 = 0.05 * jax.random.normal(jax.random.fold_in(_tk, 500 + 36), (1250, 64), jnp.float32)
        tbl_37 = 0.05 * jax.random.normal(jax.random.fold_in(_tk, 500 + 37), (1000, 64), jnp.float32)
        tbl_38 = 0.05 * jax.random.normal(jax.random.fold_in(_tk, 500 + 38), (1000, 64), jnp.float32)
        tbl_39 = 0.05 * jax.random.normal(jax.random.fold_in(_tk, 500 + 39), (1000, 64), jnp.float32)
        _rk = jax.random.fold_in(_tk, 7)
        W_top1 = 0.0354441 * jax.random.normal(jax.random.fold_in(_tk, 801), (796, 512), jnp.float32)
        W_top2 = 0.0441942 * jax.random.normal(jax.random.fold_in(_tk, 802), (512, 256), jnp.float32)
        W_top3 = 0.0625 * jax.random.normal(jax.random.fold_in(_tk, 803), (256, 1), jnp.float32)
        b_top1 = jnp.zeros((512,), jnp.float32)
        b_top2 = jnp.zeros((256,), jnp.float32)
        return (dense_ctx, ids, tbl_0, tbl_1, tbl_2, tbl_3, tbl_4, tbl_5, tbl_6, tbl_7, tbl_8, tbl_9, tbl_10, tbl_11, tbl_12, tbl_13, tbl_14, tbl_15, tbl_16, tbl_17, tbl_18, tbl_19, tbl_20, tbl_21, tbl_22, tbl_23, tbl_24, tbl_25, tbl_26, tbl_27, tbl_28, tbl_29, tbl_30, tbl_31, tbl_32, tbl_33, tbl_34, tbl_35, tbl_36, tbl_37, tbl_38, tbl_39, W_top1, b_top1, W_top2, b_top2, W_top3)
    dense_ctx, ids, tbl_0, tbl_1, tbl_2, tbl_3, tbl_4, tbl_5, tbl_6, tbl_7, tbl_8, tbl_9, tbl_10, tbl_11, tbl_12, tbl_13, tbl_14, tbl_15, tbl_16, tbl_17, tbl_18, tbl_19, tbl_20, tbl_21, tbl_22, tbl_23, tbl_24, tbl_25, tbl_26, tbl_27, tbl_28, tbl_29, tbl_30, tbl_31, tbl_32, tbl_33, tbl_34, tbl_35, tbl_36, tbl_37, tbl_38, tbl_39, W_top1, b_top1, W_top2, b_top2, W_top3 = _rec_inputs()

    def _L0_rec_setup():
        import jax, jax.numpy as jnp
        import numpy as np

        def _pair_indices(num_fields):
            i_idx, j_idx = np.triu_indices(num_fields, k=1)
            return (jnp.asarray(i_idx), jnp.asarray(j_idx))
        key = jax.random.key(seed)
        k1, k2 = jax.random.split(key)
        B, F, D = (256, 40, 64)
        P = F * (F - 1) // 2
        x = jax.random.normal(k1, (B, F, D), dtype=jnp.float32)
        W = jax.random.normal(k2, (P, D, D), dtype=jnp.float32) * (1.0 / np.sqrt(D))
        return {'x': x, 'W': W}
    _L0_rec_all = _L0_rec_setup()
    _L0_rec_in = {k: v for k, v in _L0_rec_all.items() if k in ('W',)}
    del _L0_rec_all
    return {'dense_ctx': dense_ctx, 'ids': ids, 'tbl_0': tbl_0, 'tbl_1': tbl_1, 'tbl_2': tbl_2, 'tbl_3': tbl_3, 'tbl_4': tbl_4, 'tbl_5': tbl_5, 'tbl_6': tbl_6, 'tbl_7': tbl_7, 'tbl_8': tbl_8, 'tbl_9': tbl_9, 'tbl_10': tbl_10, 'tbl_11': tbl_11, 'tbl_12': tbl_12, 'tbl_13': tbl_13, 'tbl_14': tbl_14, 'tbl_15': tbl_15, 'tbl_16': tbl_16, 'tbl_17': tbl_17, 'tbl_18': tbl_18, 'tbl_19': tbl_19, 'tbl_20': tbl_20, 'tbl_21': tbl_21, 'tbl_22': tbl_22, 'tbl_23': tbl_23, 'tbl_24': tbl_24, 'tbl_25': tbl_25, 'tbl_26': tbl_26, 'tbl_27': tbl_27, 'tbl_28': tbl_28, 'tbl_29': tbl_29, 'tbl_30': tbl_30, 'tbl_31': tbl_31, 'tbl_32': tbl_32, 'tbl_33': tbl_33, 'tbl_34': tbl_34, 'tbl_35': tbl_35, 'tbl_36': tbl_36, 'tbl_37': tbl_37, 'tbl_38': tbl_38, 'tbl_39': tbl_39, 'W_top1': W_top1, 'b_top1': b_top1, 'W_top2': W_top2, 'b_top2': b_top2, 'W_top3': W_top3, 'L0_rec_W': _L0_rec_in['W']}

def reference(dense_ctx, ids, tbl_0, tbl_1, tbl_2, tbl_3, tbl_4, tbl_5, tbl_6, tbl_7, tbl_8, tbl_9, tbl_10, tbl_11, tbl_12, tbl_13, tbl_14, tbl_15, tbl_16, tbl_17, tbl_18, tbl_19, tbl_20, tbl_21, tbl_22, tbl_23, tbl_24, tbl_25, tbl_26, tbl_27, tbl_28, tbl_29, tbl_30, tbl_31, tbl_32, tbl_33, tbl_34, tbl_35, tbl_36, tbl_37, tbl_38, tbl_39, W_top1, b_top1, W_top2, b_top2, W_top3, L0_rec_W):
    import jax
    import jax.numpy as jnp

    def _L0_rec_ref(x, W):
        import jax, jax.numpy as jnp
        import numpy as np

        def _pair_indices(num_fields):
            i_idx, j_idx = np.triu_indices(num_fields, k=1)
            return (jnp.asarray(i_idx), jnp.asarray(j_idx))
        B, F, D = x.shape
        i_idx, j_idx = _pair_indices(F)
        vi = x[:, i_idx, :]
        vj = x[:, j_idx, :]
        viW = jnp.einsum('bpd,pde->bpe', vi, W)
        out = jnp.einsum('bpe,bpe->bp', viW, vj)
        return out
    e = jnp.stack([tbl_0[ids[:, 0]], tbl_1[ids[:, 1]], tbl_2[ids[:, 2]], tbl_3[ids[:, 3]], tbl_4[ids[:, 4]], tbl_5[ids[:, 5]], tbl_6[ids[:, 6]], tbl_7[ids[:, 7]], tbl_8[ids[:, 8]], tbl_9[ids[:, 9]], tbl_10[ids[:, 10]], tbl_11[ids[:, 11]], tbl_12[ids[:, 12]], tbl_13[ids[:, 13]], tbl_14[ids[:, 14]], tbl_15[ids[:, 15]], tbl_16[ids[:, 16]], tbl_17[ids[:, 17]], tbl_18[ids[:, 18]], tbl_19[ids[:, 19]], tbl_20[ids[:, 20]], tbl_21[ids[:, 21]], tbl_22[ids[:, 22]], tbl_23[ids[:, 23]], tbl_24[ids[:, 24]], tbl_25[ids[:, 25]], tbl_26[ids[:, 26]], tbl_27[ids[:, 27]], tbl_28[ids[:, 28]], tbl_29[ids[:, 29]], tbl_30[ids[:, 30]], tbl_31[ids[:, 31]], tbl_32[ids[:, 32]], tbl_33[ids[:, 33]], tbl_34[ids[:, 34]], tbl_35[ids[:, 35]], tbl_36[ids[:, 36]], tbl_37[ids[:, 37]], tbl_38[ids[:, 38]], tbl_39[ids[:, 39]]], axis=1)
    z = _L0_rec_ref(e, L0_rec_W)
    z = z.reshape(z.shape[0], -1)
    h = jnp.concatenate([z, dense_ctx], axis=1)
    h = jnp.maximum(h @ W_top1 + b_top1, 0.0)
    h = jnp.maximum(h @ W_top2 + b_top2, 0.0)
    y = h @ W_top3
    return y

_drawn_inputs = setup_inputs


def setup_inputs(seed=0):
    import zlib

    import numpy as np

    out = dict(_drawn_inputs(seed))
    spreads = {'b_top1': (0.0, 0.1), 'b_top2': (0.0, 0.1)}
    factors = {}
    for name, (base, spread) in spreads.items():
        noise = np.random.default_rng([zlib.crc32(name.encode()), seed]).standard_normal(out[name].shape)
        drawn = base * np.exp(spread * noise) if base else spread * noise
        out[name] = jnp.asarray(drawn.astype(out[name].dtype))
    for name, factor in factors.items():
        out[name] = (out[name] * factor).astype(out[name].dtype)
    return out
```

```python
from contextlib import ExitStack

import numpy as np

import concourse.bass as bass
from concourse import mybir

P = 128
FIELDS = 40
D = 64
BATCH = 512
COUPLES = FIELDS // 2
TILES = COUPLES * COUPLES
DENSE = 16

SLOT_TILES = 2
SLOTS = TILES // SLOT_TILES
GROUP_TILES = 4
GROUPS = TILES // GROUP_TILES
GROUP_SLOTS = GROUP_TILES // SLOT_TILES
CHUNK_TILES = 8
CHUNKS = TILES // CHUNK_TILES
CHUNK_SLOTS = CHUNK_TILES // SLOT_TILES
CHUNK_COLS = CHUNK_TILES * P
Z_TILES = 64
Z_COUNT = -(-TILES // Z_TILES)
Z_GROUPS = Z_TILES // GROUP_TILES
QUAD = 32
DENSE_ROW = 3 * QUAD

H1, H2 = 512, 256
H1_TILES, H2_TILES = H1 // P, H2 // P
BATCH_TILES = BATCH // P

GATHER_RING = 4
PARTNER_RING = 4
RAW_RING = 3
SPLIT_RING = 4
U_RING = 2
PROD_RING = 4
T_RING = 2
Z_RING = 2

REDUCE_LAG = 4
LEAD_TILES = 6
LEAD_FROM = 7
GATHER_AHEAD = 2
VECTOR_CHUNKS = 12

F32 = mybir.dt.float32
F32R = mybir.dt.float32r
I32 = mybir.dt.int32
ALU = mybir.AluOpType
ACT = mybir.ActivationFunctionType


def couple_of(t):
    m = 0
    while (m + 1) * (m + 1) <= t:
        m += 1
    return m


def z_place(t):
    k, n = divmod(t, Z_TILES)
    groups = 4 if k < Z_COUNT - 1 else 3
    return k, n % groups, n // groups


def transposes_at(m):
    lead = LEAD_TILES if m >= LEAD_FROM else 0
    return max((m - 1) ** 2 if m else 0, m * m - lead)


def tower(nc, dense_t, ids, tables, w_pairs, w1, b1, w2, b2, w3, y):
    with ExitStack() as ctx:
        def sb(name, shape, dt=F32):
            return ctx.enter_context(nc.sbuf_tensor(name, shape, dt))

        def ps(name, shape):
            return ctx.enter_context(nc.psum_tensor(name, shape, F32))

        def sem(name):
            return ctx.enter_context(nc.semaphore(name))

        ids_sb = sb("ids_sb", [P, BATCH_TILES, FIELDS], I32)
        gathered = sb("gathered", [P, GATHER_RING, BATCH_TILES, 2 * D])
        partner = sb("partner", [P, PARTNER_RING, BATCH])
        mover = sb("mover", [P, FIELDS - 1, BATCH], F32R)
        w_raw = sb("w_raw", [P, RAW_RING, CHUNK_COLS])
        w_high = sb("w_high", [P, SPLIT_RING, CHUNK_COLS], F32R)
        w_low = sb("w_low", [P, SPLIT_RING, CHUNK_COLS], F32R)
        prod = sb("prod", [P, PROD_RING, SLOT_TILES, BATCH])
        z_sb = sb("z_sb", [P, Z_COUNT, BATCH])
        w1_sb = sb("w1_sb", [P, Z_COUNT, H1])
        w2_sb = sb("w2_sb", [P, H1_TILES, H2])
        w3_sb = sb("w3_sb", [P, H2_TILES])
        b1_sb = sb("b1_sb", [P, H1_TILES])
        b2_sb = sb("b2_sb", [P, H2_TILES])
        h1_sb = sb("h1_sb", [P, H1_TILES, BATCH])
        h2_sb = sb("h2_sb", [P, H2_TILES, BATCH])
        y_sb = sb("y_sb", [1, BATCH])
        identity = sb("identity", [P, P])
        selector = sb("selector", [P, 2 * QUAD - 2])

        u_ps = ps("u_ps", [P, U_RING * SLOT_TILES, BATCH])
        z_ps = ps("z_ps", [P, Z_RING, BATCH])
        t_ps = ps("t_ps", [P, T_RING, BATCH])

        last_z = (Z_COUNT - 1) % Z_RING
        h1_ps = [t_ps[:, 0, :], t_ps[:, 1, :], z_ps[:, 1 - last_z, :], u_ps[:, 0, :]]
        h2_ps = [u_ps[:, 1, :], u_ps[:, 2, :]]
        y_ps = u_ps[0:1, 3, :]

        ids_loaded = sem("ids_loaded")
        mlp_loaded = sem("mlp_loaded")
        dense_loaded = sem("dense_loaded")
        gather_landed = [sem(f"gather_landed{r}") for r in range(GATHER_RING)]
        w_loaded = [sem(f"w_loaded{r}") for r in range(RAW_RING)]
        identity_zeroed = sem("identity_zeroed")
        identity_ready = sem("identity_ready")
        selector_zeroed = sem("selector_zeroed")
        selector_ready = sem("selector_ready")
        dense_zeroed = sem("dense_zeroed")
        transposed = sem("transposed")
        partner_ready = sem("partner_ready")
        high_ready = sem("high_ready")
        low_ready = sem("low_ready")
        w_high_ready = sem("w_high_ready")
        w_low_vector = sem("w_low_vector")
        w_low_gpsimd = sem("w_low_gpsimd")
        u_ready = sem("u_ready")
        prod_ready = sem("prod_ready")
        sums_ready = sem("sums_ready")
        z_ready = sem("z_ready")
        h1_summed = sem("h1_summed")
        h1_ready = sem("h1_ready")
        h2_summed = sem("h2_summed")
        h2_ready = sem("h2_ready")
        y_summed = sem("y_summed")
        y_ready = sem("y_ready")
        y_stored = sem("y_stored")

        block = ctx.enter_context(nc.Block())

        def wait_low(eng, c):
            if c < VECTOR_CHUNKS:
                eng.wait_ge(w_low_vector, c + 1)
            else:
                eng.wait_ge(w_low_gpsimd, c - VECTOR_CHUNKS + 1)

        def slots_through_couple(m):
            return ((m + 1) ** 2 - 1) // SLOT_TILES + 1

        def chunk_at(c):
            return CHUNK_TILES * (c - SPLIT_RING + 1)

        split_steps = [(chunk_at(c), "split", c) for c in range(CHUNKS)]

        @block.sync
        def _(sp):
            sp.dma_start(ids_sb[:], ids.rearrange("(t p) f -> p t f", p=P)).then_inc(ids_loaded, 16)
            for c in range(CHUNKS):
                if c >= RAW_RING:
                    sp.wait_ge(w_high_ready, c - RAW_RING + 1)
                    wait_low(sp, c - RAW_RING)
                for half in range(2):
                    sp.dma_start(w_raw[half * D:(half + 1) * D, c % RAW_RING, :],
                                 w_pairs[c]).then_inc(w_loaded[c % RAW_RING], 16)
                if c == RAW_RING + 1:
                    sp.dma_start(w1_sb[:], w1.rearrange("k p n -> p k n")).then_inc(mlp_loaded, 16)
                    sp.dma_start(w2_sb[:], w2.rearrange("(k p) n -> p k n", p=P)).then_inc(mlp_loaded, 16)
                    sp.dma_start(w3_sb[:], w3).then_inc(mlp_loaded, 16)
                    sp.dma_start(b1_sb[:], b1).then_inc(mlp_loaded, 16)
                    sp.dma_start(b2_sb[:], b2).then_inc(mlp_loaded, 16)
                    sp.wait_ge(dense_zeroed, 1)
                    sp.dma_start(z_sb[DENSE_ROW:DENSE_ROW + DENSE, Z_COUNT - 1, :],
                                 dense_t).then_inc(dense_loaded, 16)
            sp.wait_ge(y_ready, 1)
            sp.dma_start(y.rearrange("b o -> o b"), y_sb[:]).then_inc(y_stored, 16)
            sp.wait_ge(y_stored, 16)

        @block.gpsimd
        def _(pool):
            def gather(m):
                if m >= GATHER_RING:
                    pool.wait_ge(transposed, m - GATHER_RING + 1)
                for f in range(2 * m, 2 * m + 2):
                    for bt in range(BATCH_TILES):
                        nc.gpsimd.indirect_dma_start(
                            out=gathered[:, m % GATHER_RING, bt, (f % 2) * D:(f % 2 + 1) * D],
                            out_offset=None,
                            in_=tables[f],
                            in_offset=bass.IndirectOffsetOnAxis(ap=ids_sb[:, bt, f:f + 1], axis=0),
                        ).then_inc(gather_landed[m % GATHER_RING], 16)

            def make_low(c):
                pool.wait_ge(w_high_ready, c + 1)
                nc.gpsimd.tensor_tensor(w_low[:, c % SPLIT_RING, :], w_raw[:, c % RAW_RING, :],
                                        w_high[:, c % SPLIT_RING, :].bitcast(F32),
                                        ALU.subtract).then_inc(w_low_gpsimd, 1)

            nc.gpsimd.memset(identity[:], 0.0).then_inc(identity_zeroed, 1)
            pool.wait_ge(identity_zeroed, 1)
            nc.gpsimd.affine_select(out=identity[:], in_=identity[:], compare_op=ALU.not_equal, fill=1.0,
                                    base=0, pattern=[[-1, P]], channel_multiplier=1).then_inc(identity_ready, 1)
            pool.wait_ge(ids_loaded, 16)
            steps = [(transposes_at(max(m - GATHER_AHEAD, 0)) - 1, "gather", m) for m in range(COUPLES)]
            steps += [s for s in split_steps if s[2] >= VECTOR_CHUNKS]
            for _, what, n in sorted(steps, key=lambda s: s[0]):
                if what == "gather":
                    gather(n)
                else:
                    make_low(n)

        @block.scalar
        def _(act):
            def make_high(c):
                act.wait_ge(w_loaded[c % RAW_RING], 32 * (c // RAW_RING + 1))
                if c >= SPLIT_RING:
                    act.wait_ge(u_ready, CHUNK_SLOTS * (c - SPLIT_RING + 1))
                nc.scalar.copy(w_high[:, c % SPLIT_RING, :], w_raw[:, c % RAW_RING, :]).then_inc(w_high_ready, 1)

            def take_couple(m):
                act.wait_ge(transposed, m + 1)
                if m >= PARTNER_RING:
                    act.wait_ge(prod_ready, slots_through_couple(m - PARTNER_RING))
                    act.wait_ge(low_ready, m - PARTNER_RING + 1)
                t = t_ps[:, m % T_RING, :]
                nc.scalar.copy(partner[:, m % PARTNER_RING, :], t).then_inc(partner_ready, 1)
                nc.scalar.copy(mover[0:D, 2 * m, :], t[0:D, :]).then_inc(high_ready, 1)
                if 2 * m + 1 < FIELDS - 1:
                    nc.scalar.copy(mover[D:P, 2 * m + 1, :], t[D:P, :]).then_inc(high_ready, 1)

            def take_z(k):
                act.wait_ge(sums_ready, min(Z_GROUPS * (k + 1), GROUPS))
                rows = P if k < Z_COUNT - 1 else DENSE_ROW
                nc.scalar.copy(z_sb[0:rows, k, :], z_ps[0:rows, k % Z_RING, :]).then_inc(z_ready, 1)

            steps = list(split_steps)
            steps += [(transposes_at(m) + 0.5, "couple", m) for m in range(COUPLES)]
            steps += [(Z_TILES * (k + 1) + SLOT_TILES * REDUCE_LAG, "z", k) for k in range(Z_COUNT - 1)]
            for _, what, n in sorted(steps, key=lambda s: s[0]):
                if what == "split":
                    make_high(n)
                elif what == "couple":
                    take_couple(n)
                else:
                    take_z(n)
            take_z(Z_COUNT - 1)

            act.wait_ge(mlp_loaded, 5 * 16)
            for n in range(H1_TILES):
                act.wait_ge(h1_summed, n + 1)
                nc.scalar.activation(h1_sb[:, n, :], h1_ps[n], ACT.Relu, bias=b1_sb[:, n:n + 1]).then_inc(h1_ready, 1)
            for n in range(H2_TILES):
                act.wait_ge(h2_summed, n + 1)
                nc.scalar.activation(h2_sb[:, n, :], h2_ps[n], ACT.Relu, bias=b2_sb[:, n:n + 1]).then_inc(h2_ready, 1)
            act.wait_ge(y_summed, 1)
            nc.scalar.copy(y_sb[:], y_ps).then_inc(y_ready, 1)

        @block.vector
        def _(dve):
            def multiply(s):
                first, last = (couple_of(t) for t in (SLOT_TILES * s, SLOT_TILES * s + 1))
                dve.wait_ge(partner_ready, last + 1)
                dve.wait_ge(u_ready, s + 1)
                if s >= PROD_RING:
                    dve.wait_ge(sums_ready, (s - PROD_RING) // GROUP_SLOTS + 1)
                r = first % PARTNER_RING
                if first == last:
                    by = partner[:, r, :].unsqueeze(1).to_broadcast([P, SLOT_TILES, BATCH])
                else:
                    by = partner[:, r:r + 2, :]
                u = SLOT_TILES * (s % U_RING)
                nc.vector.tensor_tensor(prod[:, s % PROD_RING, :, :], u_ps[:, u:u + SLOT_TILES, :], by,
                                        ALU.mult).then_inc(prod_ready, 1)

            def make_mover_low(m):
                dve.wait_ge(high_ready, min(2 * (m + 1), FIELDS - 1))
                raw = partner[:, m % PARTNER_RING, :]
                low = nc.vector.tensor_tensor(mover[D:P, 2 * m, :], raw[0:D, :],
                                              mover[0:D, 2 * m, :].bitcast(F32), ALU.subtract)
                if 2 * m + 1 < FIELDS - 1:
                    low = nc.vector.tensor_tensor(mover[0:D, 2 * m + 1, :], raw[D:P, :],
                                                  mover[D:P, 2 * m + 1, :].bitcast(F32), ALU.subtract)
                low.then_inc(low_ready, 1)

            def make_low(c):
                dve.wait_ge(w_high_ready, c + 1)
                nc.vector.tensor_tensor(w_low[:, c % SPLIT_RING, :], w_raw[:, c % RAW_RING, :],
                                        w_high[:, c % SPLIT_RING, :].bitcast(F32),
                                        ALU.subtract).then_inc(w_low_vector, 1)

            nc.vector.memset(selector[:], 0.0).then_inc(selector_zeroed, 1)
            dve.wait_ge(selector_zeroed, 1)
            for q in range(2):
                nc.vector.memset(selector[q * D:(q + 1) * D, QUAD - 2 + q:QUAD - 1 + q], 1.0).then_inc(selector_ready, 1)
            nc.vector.memset(z_sb[DENSE_ROW:P, Z_COUNT - 1, :], 0.0).then_inc(dense_zeroed, 1)

            steps = [s for s in split_steps if s[2] < VECTOR_CHUNKS]
            steps += [(transposes_at(m) + 0.6, "low", m) for m in range(COUPLES)]
            steps += [(SLOT_TILES * (s + 1), "multiply", s) for s in range(SLOTS)]
            for _, what, n in sorted(steps, key=lambda s: s[0]):
                if what == "split":
                    make_low(n)
                elif what == "low":
                    make_mover_low(n)
                else:
                    multiply(n)

        @block.tensor
        def _(pe):
            def transpose_couple(m):
                pe.wait_ge(gather_landed[m % GATHER_RING], 2 * BATCH_TILES * 16 * (m // GATHER_RING + 1))
                if m >= T_RING:
                    pe.wait_ge(high_ready, 2 * (m - T_RING + 1))
                for bt in range(BATCH_TILES):
                    last = nc.tensor.transpose(t_ps[:, m % T_RING, bt * P:(bt + 1) * P],
                                               gathered[:, m % GATHER_RING, bt, :], identity[:])
                last.then_inc(transposed, 1)

            def multiply(t):
                m = couple_of(t)
                i = t - m * m
                c, n = divmod(t, CHUNK_TILES)
                s, k = divmod(t, SLOT_TILES)
                if n == 0:
                    pe.wait_ge(w_high_ready, c + 1)
                    wait_low(pe, c)
                if i == 2 * m:
                    pe.wait_ge(low_ready, m + 1)
                if k == 0 and s >= U_RING:
                    pe.wait_ge(prod_ready, s - U_RING + 1)
                out = u_ps[:, SLOT_TILES * (s % U_RING) + k, :]
                cols = slice(n * P, (n + 1) * P)
                nc.tensor.matmul(out, w_high[:, c % SPLIT_RING, cols], mover[:, i, :], start=True, stop=False)
                last = nc.tensor.matmul(out, w_low[:, c % SPLIT_RING, cols], mover[:, i, :], start=False, stop=True)
                if k == SLOT_TILES - 1:
                    last.then_inc(u_ready, 1)

            def sum_group(g):
                pe.wait_ge(prod_ready, GROUP_SLOTS * (g + 1))
                for t in range(GROUP_TILES * g, GROUP_TILES * (g + 1)):
                    k, q, r = z_place(t)
                    if t % Z_TILES == 0 and k >= Z_RING:
                        pe.wait_ge(z_ready, k - Z_RING + 1)
                    final = r == z_rows[k, q] - 1
                    at = QUAD - 2 - 2 * r
                    last = nc.tensor.matmul(z_ps[QUAD * q:QUAD * (q + 1), k % Z_RING, :],
                                            selector[:, at:at + QUAD],
                                            prod[:, t // SLOT_TILES % PROD_RING, t % SLOT_TILES, :],
                                            start=(r == 0), stop=final)
                last.then_inc(sums_ready, 1)

            def layer1(k, n):
                return nc.tensor.matmul(h1_ps[n], w1_sb[:, k, n * P:(n + 1) * P], z_sb[:, k, :],
                                        start=(k == 0), stop=(k == Z_COUNT - 1))

            z_rows = {}
            for t in range(TILES):
                k, q, r = z_place(t)
                z_rows[k, q] = r + 1
            transpose_before = {}
            for m in range(COUPLES):
                transpose_before.setdefault(transposes_at(m), []).append(m)

            pe.wait_ge(identity_ready, 1)
            for t in range(TILES):
                for m in transpose_before.get(t, []):
                    transpose_couple(m)
                multiply(t)
                done = (t + 1) // SLOT_TILES - REDUCE_LAG
                if (t + 1) % GROUP_TILES == 0 and done >= 0:
                    if done == 0:
                        pe.wait_ge(selector_ready, 2)
                    sum_group(done // GROUP_SLOTS)

            pe.wait_ge(mlp_loaded, 5 * 16)
            pe.wait_ge(high_ready, FIELDS - 1)
            pe.wait_ge(z_ready, Z_COUNT - 1)
            for n in range(2):
                for k in range(Z_COUNT - 1):
                    layer1(k, n)
            sum_group(GROUPS - 1)
            for n in range(2, H1_TILES):
                for k in range(Z_COUNT - 1):
                    layer1(k, n)
            pe.wait_ge(dense_loaded, 16)
            pe.wait_ge(z_ready, Z_COUNT)
            for n in range(H1_TILES):
                layer1(Z_COUNT - 1, n).then_inc(h1_summed, 1)
            for k in range(H1_TILES):
                pe.wait_ge(h1_ready, k + 1)
                for n in range(H2_TILES):
                    last = nc.tensor.matmul(h2_ps[n], w2_sb[:, k, n * P:(n + 1) * P], h1_sb[:, k, :],
                                            start=(k == 0), stop=(k == H1_TILES - 1))
                    if k == H1_TILES - 1:
                        last.then_inc(h2_summed, 1)
            for k in range(H2_TILES):
                pe.wait_ge(h2_ready, k + 1)
                last = nc.tensor.matmul(y_ps, w3_sb[:, k:k + 1], h2_sb[:, k, :],
                                        start=(k == 0), stop=(k == H2_TILES - 1))
            last.then_inc(y_summed, 1)


def pair_index(i, j):
    return i * FIELDS - i * (i + 1) // 2 + j - i - 1


def kernel(**inputs):
    import concourse.bacc as bacc
    from concourse.bass_utils import run_bass_kernel_spmd

    w = np.asarray(inputs["L0_rec_W"])
    w_tiles = np.zeros((TILES, 2, D, D), w.dtype)
    w1 = np.asarray(inputs["W_top1"])
    w1_rows = np.zeros((Z_COUNT, P, H1), w1.dtype)
    for t in range(TILES):
        m = couple_of(t)
        i = t - m * m
        k, q, r = z_place(t)
        for side in range(2):
            j = 2 * m + side
            if i < j:
                w_tiles[t, side] = w[pair_index(i, j)]
                w1_rows[k, QUAD * q + 2 * r + side] = w1[pair_index(i, j)]
    w1_rows[Z_COUNT - 1, DENSE_ROW:DENSE_ROW + DENSE] = w1[-DENSE:]
    w_pairs = w_tiles.reshape(CHUNKS, CHUNK_TILES, 2, D, D).transpose(0, 3, 1, 2, 4).reshape(CHUNKS, D, CHUNK_COLS)

    arrays = {
        "dense_t": np.asarray(inputs["dense_ctx"]).T,
        "ids": np.asarray(inputs["ids"]),
        "w_pairs": w_pairs,
        "w1": w1_rows,
        "b1": np.asarray(inputs["b_top1"]).reshape(H1_TILES, P).T,
        "w2": np.asarray(inputs["W_top2"]),
        "b2": np.asarray(inputs["b_top2"]).reshape(H2_TILES, P).T,
        "w3": np.asarray(inputs["W_top3"]).reshape(H2_TILES, P).T,
    }
    for f in range(FIELDS):
        arrays[f"tbl_{f}"] = np.asarray(inputs[f"tbl_{f}"])
    arrays = {f"in_{name}": np.ascontiguousarray(a) for name, a in arrays.items()}

    nc = bacc.Bacc("TRN2", target_bir_lowering=False, num_devices=1)
    ap = {
        name[3:]: nc.dram_tensor(name, a.shape, mybir.dt.from_np(a.dtype), kind="ExternalInput").ap()
        for name, a in arrays.items()
    }
    y = nc.dram_tensor("out_y", (BATCH, 1), F32, kind="ExternalOutput").ap()
    tower(nc, ap["dense_t"], ap["ids"], [ap[f"tbl_{f}"] for f in range(FIELDS)], ap["w_pairs"],
          ap["w1"], ap["b1"], ap["w2"], ap["b2"], ap["w3"], y)
    result = run_bass_kernel_spmd(nc, [arrays], core_ids=[0])
    return result.results[0]["out_y"]
```

```python
from contextlib import ExitStack

import numpy as np

import concourse.bass as bass
from concourse import mybir

P = 128
FIELDS = 40
D = 64
BATCH = 512
COUPLES = FIELDS // 2
TILES = COUPLES * COUPLES
DENSE = 16

SLOT_TILES = 2
SLOTS = TILES // SLOT_TILES
GROUP_TILES = 4
GROUPS = TILES // GROUP_TILES
GROUP_SLOTS = GROUP_TILES // SLOT_TILES
CHUNK_TILES = 8
CHUNKS = TILES // CHUNK_TILES
CHUNK_SLOTS = CHUNK_TILES // SLOT_TILES
CHUNK_COLS = CHUNK_TILES * P
Z_TILES = 64
Z_COUNT = -(-TILES // Z_TILES)
Z_GROUPS = Z_TILES // GROUP_TILES
QUAD = 32
DENSE_ROW = 3 * QUAD

H1, H2 = 512, 256
H1_TILES, H2_TILES = H1 // P, H2 // P
BATCH_TILES = BATCH // P

GATHER_RING = 4
PARTNER_RING = 4
RAW_RING = 3
SPLIT_RING = 4
U_RING = 3
PROD_RING = 6
Z_RING = 1
HOT_RING = 2

HOT_COUPLES = (0, 2)
HOT_ROWS = 1000
HOT_TILES = 8
HOT_P = HOT_ROWS // HOT_TILES
HOT_LEAD = 20

SUM_LAG = 6
LEAD_TILES = 6
LEAD_FROM = 7
GATHER_AHEAD = 2
SPLIT_LEAD = 18
LOW_LATE = 1
LOW_PARTS = 2
GPSIMD_FROM = 8
GPSIMD_EVERY = 1

F32 = mybir.dt.float32
F32R = mybir.dt.float32r
I32 = mybir.dt.int32
ALU = mybir.AluOpType
ACT = mybir.ActivationFunctionType


def couple_of(t):
    m = 0
    while (m + 1) * (m + 1) <= t:
        m += 1
    return m


def z_place(t):
    k, n = divmod(t, Z_TILES)
    groups = 4 if k < Z_COUNT - 1 else 3
    return k, n % groups, n // groups


def hot_number(q):
    return 2 * HOT_COUPLES.index(q // 2) + q % 2


def gather_number(m):
    return sum(x not in HOT_COUPLES for x in range(m))


def by_gpsimd(c):
    return c >= GPSIMD_FROM and (c - GPSIMD_FROM) % GPSIMD_EVERY == 0


def low_count(c):
    return sum(by_gpsimd(x) == by_gpsimd(c) for x in range(c + 1))


def transposes_at(m):
    lead = LEAD_TILES if m >= LEAD_FROM else 0
    return max((m - 1) ** 2 if m else 0, m * m - lead)


def bank_steps():
    steps = []
    for m in range(COUPLES):
        at = transposes_at(m)
        if m in HOT_COUPLES:
            steps += [(at - 2, "hot", 2 * m), (at - 1, "hot", 2 * m + 1), (at - 0.5, "pair", m)]
        else:
            steps.append((at, "couple", m))
    return sorted(steps)


def tower(nc, dense_t, ids, ids_t, tables, w_pairs, w1, b1, w2, b2, w3, y):
    with ExitStack() as ctx:
        def sb(name, shape, dt=F32):
            return ctx.enter_context(nc.sbuf_tensor(name, shape, dt))

        def ps(name, shape):
            return ctx.enter_context(nc.psum_tensor(name, shape, F32))

        def sem(name):
            return ctx.enter_context(nc.semaphore(name))

        ids_sb = sb("ids_sb", [P, BATCH_TILES, FIELDS], I32)
        gathered = sb("gathered", [P, GATHER_RING, BATCH_TILES, 2 * D])
        partner = sb("partner", [P, PARTNER_RING, BATCH])
        mover = sb("mover", [P, FIELDS - 1, BATCH], F32R)
        w_raw = sb("w_raw", [P, RAW_RING, CHUNK_COLS])
        w_high = sb("w_high", [P, SPLIT_RING, CHUNK_COLS], F32R)
        w_low = sb("w_low", [P, SPLIT_RING, CHUNK_COLS], F32R)
        prod = sb("prod", [P, PROD_RING, SLOT_TILES, BATCH])
        z_sb = sb("z_sb", [P, Z_COUNT, BATCH])
        w1_sb = sb("w1_sb", [P, Z_COUNT, H1])
        w2_sb = sb("w2_sb", [P, H1_TILES, H2])
        w3_sb = sb("w3_sb", [P, H2_TILES])
        b1_sb = sb("b1_sb", [P, H1_TILES])
        b2_sb = sb("b2_sb", [P, H2_TILES])
        hidden = w_raw[:].rearrange("p r c -> p (r c)").rearrange("p (n b) -> p n b", b=BATCH)
        h1_sb = hidden[:, 0:H1_TILES, :]
        h2_sb = hidden[:, H1_TILES:H1_TILES + H2_TILES, :]
        y_sb = sb("y_sb", [1, BATCH])
        halves_sum = sb("halves_sum", [P, 3 * D], F32R)
        hot_row = sb("hot_row", [P, HOT_TILES])
        hot_row_int = sb("hot_row_int", [P, HOT_TILES], I32)
        hot_table = z_sb[:, 0:HOT_RING, :]
        hot_ids = z_sb[:, HOT_RING:2 * HOT_RING, :].bitcast(I32)
        top = FIELDS - 1
        one_hot = [mover[:, top - HOT_TILES * (r + 1):top - HOT_TILES * r, :] for r in range(HOT_RING)]
        top -= HOT_TILES * HOT_RING
        hot_split = [mover[:, top - 2 * (r + 1):top - 2 * r, :].rearrange("p a (k c) -> p (a k) c", c=2 * D)
                     for r in range(HOT_RING)]
        identity = sb("identity", [P, P])
        selector = sb("selector", [P, 2 * QUAD - 2])

        u_ps = ps("u_ps", [P, U_RING * SLOT_TILES, BATCH])
        z_ps = ps("z_ps", [P, Z_RING, BATCH])
        t_ps = ps("t_ps", [P, BATCH])

        tail = [(s, u_ps[:, SLOT_TILES * (s % U_RING) + k, :]) for s in range(SLOTS - U_RING, SLOTS)
                for k in range(SLOT_TILES)]
        h1_ps = [t_ps[:, :]] + [bank for _, bank in tail[:3]]
        left_at = [0] + [s + 1 for s, _ in tail[:3]]
        h2_ps = [tail[3][1], tail[4][1]]
        y_ps = tail[5][1][0:1, :]

        ids_loaded = sem("ids_loaded")
        mlp_loaded = sem("mlp_loaded")
        dense_loaded = sem("dense_loaded")
        gather_landed = [sem(f"gather_landed{r}") for r in range(GATHER_RING)]
        w_loaded = [sem(f"w_loaded{r}") for r in range(RAW_RING)]
        identity_zeroed = sem("identity_zeroed")
        identity_ready = sem("identity_ready")
        selector_zeroed = sem("selector_zeroed")
        selector_ready = sem("selector_ready")
        dense_zeroed = sem("dense_zeroed")
        bank_filled = sem("bank_filled")
        bank_left = sem("bank_left")
        hot_loaded = [sem(f"hot_loaded{r}") for r in range(HOT_RING)]
        hot_rows_numbered = sem("hot_rows_numbered")
        hot_rows_ready = sem("hot_rows_ready")
        hot_high_ready = sem("hot_high_ready")
        hot_ready = sem("hot_ready")
        halves_zeroed = sem("halves_zeroed")
        halves_ready = sem("halves_ready")
        partner_ready = sem("partner_ready")
        low_ready = sem("low_ready")
        w_high_ready = sem("w_high_ready")
        w_low_vector = sem("w_low_vector")
        w_low_gpsimd = sem("w_low_gpsimd")
        u_ready = sem("u_ready")
        prod_ready = sem("prod_ready")
        sums_ready = sem("sums_ready")
        z_ready = sem("z_ready")
        h1_summed = sem("h1_summed")
        h1_ready = sem("h1_ready")
        h2_summed = sem("h2_summed")
        h2_ready = sem("h2_ready")
        y_summed = sem("y_summed")
        y_ready = sem("y_ready")
        y_stored = sem("y_stored")

        block = ctx.enter_context(nc.Block())

        def wait_low(eng, c):
            eng.wait_ge(w_low_gpsimd if by_gpsimd(c) else w_low_vector, LOW_PARTS * low_count(c))

        gathered_couples = [m for m in range(COUPLES) if m not in HOT_COUPLES]
        banked = bank_steps()
        bank_number = {(kind, n): k for k, (_, kind, n) in enumerate(banked)}

        def wait_bank_left(eng, k):
            _, kind, n = banked[k]
            if kind == "pair":
                eng.wait_ge(partner_ready, n + 1)
            else:
                eng.wait_ge(bank_left, sum(x[1] != "pair" for x in banked[:k + 1]))

        def hot_ring_left(eng, n):
            if n >= HOT_RING:
                q = 2 * HOT_COUPLES[(n - HOT_RING) // 2] + n % 2
                eng.wait_ge(bank_filled, bank_number["hot", q] + 1)

        def slots_through_couple(m):
            return ((m + 1) ** 2 - 1) // SLOT_TILES + 1

        def chunk_at(c):
            return CHUNK_TILES * c - SPLIT_LEAD

        split_steps = [(chunk_at(c), "split", c) for c in range(CHUNKS)]
        hot_steps = []
        for m in HOT_COUPLES:
            for q in (2 * m, 2 * m + 1):
                at = banked[bank_number["hot", q]][0] - HOT_LEAD
                if hot_number(q) >= HOT_RING:
                    last = hot_number(q) - HOT_RING
                    at = max(at, banked[bank_number["hot", 2 * HOT_COUPLES[last // 2] + last % 2]][0] + 0.1)
                hot_steps.append((at, "hot table", q))
        low_steps = [(chunk_at(c) + LOW_LATE * (part + 1), "split", (c, part))
                     for c in range(CHUNKS) for part in range(LOW_PARTS)]

        @block.sync
        def _(sp):
            def load_hot(q):
                n = hot_number(q)
                if n >= HOT_RING:
                    sp.wait_ge(hot_ready, n - HOT_RING + 1)
                r = n % HOT_RING
                rows = tables[q].rearrange("(p k) d -> p (k d)", k=HOT_TILES)
                for a, b in ((0, 112), (112, HOT_P)):
                    sp.dma_start(hot_table[a:b, r, :], rows[a:b, :]).then_inc(hot_loaded[r], 16)
                sp.dma_start(hot_ids[:, r, :], ids_t[q:q + 1, :].to_broadcast([P, BATCH])).then_inc(hot_loaded[r], 16)

            sp.dma_start(ids_sb[:], ids.rearrange("(t p) f -> p t f", p=P)).then_inc(ids_loaded, 16)
            hot_fields = [q for _, _, q in hot_steps]
            for q in hot_fields[:HOT_RING]:
                load_hot(q)
            for c in range(CHUNKS):
                if c >= RAW_RING:
                    sp.wait_ge(w_high_ready, c - RAW_RING + 1)
                    wait_low(sp, c - RAW_RING)
                for half in range(2):
                    sp.dma_start(w_raw[half * D:(half + 1) * D, c % RAW_RING, :],
                                 w_pairs[c]).then_inc(w_loaded[c % RAW_RING], 16)
                if c == RAW_RING - 1:
                    for q in hot_fields[HOT_RING:]:
                        load_hot(q)
                if c == RAW_RING + len(hot_fields):
                    sp.dma_start(w1_sb[:], w1.rearrange("k p n -> p k n")).then_inc(mlp_loaded, 16)
                    sp.dma_start(w2_sb[:], w2.rearrange("(k p) n -> p k n", p=P)).then_inc(mlp_loaded, 16)
                    sp.dma_start(w3_sb[:], w3).then_inc(mlp_loaded, 16)
                    sp.dma_start(b1_sb[:], b1).then_inc(mlp_loaded, 16)
                    sp.dma_start(b2_sb[:], b2).then_inc(mlp_loaded, 16)
                    sp.wait_ge(dense_zeroed, 1)
                    sp.dma_start(z_sb[DENSE_ROW:DENSE_ROW + DENSE, Z_COUNT - 1, :],
                                 dense_t).then_inc(dense_loaded, 16)
            sp.wait_ge(y_ready, 1)
            sp.dma_start(y.rearrange("b o -> o b"), y_sb[:]).then_inc(y_stored, 16)
            sp.wait_ge(y_stored, 16)

        @block.gpsimd
        def _(pool):
            def gather(m):
                r = gather_number(m) % GATHER_RING
                if gather_number(m) >= GATHER_RING:
                    last = gathered_couples[gather_number(m) - GATHER_RING]
                    pool.wait_ge(bank_filled, bank_number["couple", last] + 1)
                for f in range(2 * m, 2 * m + 2):
                    for bt in range(BATCH_TILES):
                        nc.gpsimd.indirect_dma_start(
                            out=gathered[:, r, bt, (f % 2) * D:(f % 2 + 1) * D],
                            out_offset=None,
                            in_=tables[f],
                            in_offset=bass.IndirectOffsetOnAxis(ap=ids_sb[:, bt, f:f + 1], axis=0),
                        ).then_inc(gather_landed[r], 16)

            def make_low(c, part):
                pool.wait_ge(w_high_ready, c + 1)
                cols = slice(part * CHUNK_COLS // LOW_PARTS, (part + 1) * CHUNK_COLS // LOW_PARTS)
                nc.gpsimd.tensor_tensor(w_low[:, c % SPLIT_RING, cols], w_raw[:, c % RAW_RING, cols],
                                        w_high[:, c % SPLIT_RING, cols].bitcast(F32),
                                        ALU.subtract).then_inc(w_low_gpsimd, 1)

            nc.gpsimd.memset(identity[:], 0.0).then_inc(identity_zeroed, 1)
            pool.wait_ge(identity_zeroed, 1)
            nc.gpsimd.affine_select(out=identity[:], in_=identity[:], compare_op=ALU.not_equal, fill=1.0,
                                    base=0, pattern=[[-1, P]], channel_multiplier=1).then_inc(identity_ready, 1)
            nc.gpsimd.iota(hot_row_int[:], pattern=[[1, HOT_TILES]], base=0,
                           channel_multiplier=HOT_TILES).then_inc(hot_rows_numbered, 1)
            pool.wait_ge(ids_loaded, 16)
            steps = [(transposes_at(max(m - GATHER_AHEAD, 0)) - 1, "gather", m) for m in gathered_couples]
            steps += [s for s in low_steps if by_gpsimd(s[2][0])]
            for _, what, n in sorted(steps, key=lambda s: s[0]):
                if what == "gather":
                    gather(n)
                else:
                    make_low(*n)

        @block.scalar
        def _(act):
            def make_high(c):
                act.wait_ge(w_loaded[c % RAW_RING], 32 * (c // RAW_RING + 1))
                if c >= SPLIT_RING:
                    act.wait_ge(u_ready, CHUNK_SLOTS * (c - SPLIT_RING + 1))
                nc.scalar.copy(w_high[:, c % SPLIT_RING, :], w_raw[:, c % RAW_RING, :]).then_inc(w_high_ready, 1)

            def make_hot_high(q):
                r = hot_number(q) % HOT_RING
                act.wait_ge(hot_loaded[r], 3 * 16 * (hot_number(q) // HOT_RING + 1))
                hot_ring_left(act, hot_number(q))
                nc.scalar.copy(hot_split[r][0:HOT_P, :, 0:D],
                               hot_table[0:HOT_P, r, :].rearrange("p (k d) -> p k d", d=D)).then_inc(hot_high_ready, 1)

            def take_hot(q):
                act.wait_ge(bank_filled, bank_number["hot", q] + 1)
                nc.scalar.copy(mover[:, q, :], t_ps[:, :]).then_inc(bank_left, 1)

            def take_partner(m):
                if m >= PARTNER_RING:
                    last = m - PARTNER_RING
                    act.wait_ge(prod_ready, slots_through_couple(last))
                    if last not in HOT_COUPLES:
                        act.wait_ge(low_ready, gather_number(last) + 1)
                return nc.scalar.copy(partner[:, m % PARTNER_RING, :], t_ps[:, :]).then_inc(partner_ready, 1)

            def take_pair(m):
                act.wait_ge(bank_filled, bank_number["pair", m] + 1)
                take_partner(m)

            def take_couple(m):
                act.wait_ge(bank_filled, bank_number["couple", m] + 1)
                take_partner(m)
                copy = nc.scalar.copy(mover[0:D, 2 * m, :], t_ps[0:D, :])
                if 2 * m + 1 < FIELDS - 1:
                    copy = nc.scalar.copy(mover[D:P, 2 * m + 1, :], t_ps[D:P, :])
                copy.then_inc(bank_left, 1)

            def take_z(k):
                act.wait_ge(sums_ready, min(Z_GROUPS * (k + 1), GROUPS))
                rows = P if k < Z_COUNT - 1 else DENSE_ROW
                nc.scalar.copy(z_sb[0:rows, k, :], z_ps[0:rows, k % Z_RING, :]).then_inc(z_ready, 1)

            steps = split_steps + banked + hot_steps
            steps += [(Z_TILES * (k + 1) + SLOT_TILES * (SUM_LAG - GROUP_SLOTS), "z", k) for k in range(Z_COUNT - 1)]
            for _, what, n in sorted(steps, key=lambda s: s[0]):
                if what == "split":
                    make_high(n)
                elif what == "hot table":
                    make_hot_high(n)
                elif what == "hot":
                    take_hot(n)
                elif what == "pair":
                    take_pair(n)
                elif what == "couple":
                    take_couple(n)
                else:
                    take_z(n)
            take_z(Z_COUNT - 1)

            act.wait_ge(mlp_loaded, 5 * 16)
            for n in range(H1_TILES):
                act.wait_ge(h1_summed, n + 1)
                nc.scalar.activation(h1_sb[:, n, :], h1_ps[n], ACT.Relu, bias=b1_sb[:, n:n + 1]).then_inc(h1_ready, 1)
            for n in range(H2_TILES):
                act.wait_ge(h2_summed, n + 1)
                nc.scalar.activation(h2_sb[:, n, :], h2_ps[n], ACT.Relu, bias=b2_sb[:, n:n + 1]).then_inc(h2_ready, 1)
            act.wait_ge(y_summed, 1)
            nc.scalar.copy(y_sb[:], y_ps).then_inc(y_ready, 1)

        @block.vector
        def _(dve):
            def multiply(s):
                first, last = (couple_of(t) for t in (SLOT_TILES * s, SLOT_TILES * s + 1))
                dve.wait_ge(partner_ready, last + 1)
                dve.wait_ge(u_ready, s + 1)
                if s >= PROD_RING:
                    dve.wait_ge(sums_ready, (s - PROD_RING) // GROUP_SLOTS + 1)
                r = first % PARTNER_RING
                if first == last:
                    by = partner[:, r, :].unsqueeze(1).to_broadcast([P, SLOT_TILES, BATCH])
                else:
                    by = partner[:, r:r + 2, :]
                u = SLOT_TILES * (s % U_RING)
                nc.vector.tensor_tensor(prod[:, s % PROD_RING, :, :], u_ps[:, u:u + SLOT_TILES, :], by,
                                        ALU.mult).then_inc(prod_ready, 1)

            def make_mover_low(m):
                wait_bank_left(dve, bank_number["couple", m])
                raw = partner[:, m % PARTNER_RING, :]
                low = nc.vector.tensor_tensor(mover[D:P, 2 * m, :], raw[0:D, :],
                                              mover[0:D, 2 * m, :].bitcast(F32), ALU.subtract)
                if 2 * m + 1 < FIELDS - 1:
                    low = nc.vector.tensor_tensor(mover[0:D, 2 * m + 1, :], raw[D:P, :],
                                                  mover[D:P, 2 * m + 1, :].bitcast(F32), ALU.subtract)
                low.then_inc(low_ready, 1)

            def make_low(c, part):
                dve.wait_ge(w_high_ready, c + 1)
                cols = slice(part * CHUNK_COLS // LOW_PARTS, (part + 1) * CHUNK_COLS // LOW_PARTS)
                nc.vector.tensor_tensor(w_low[:, c % SPLIT_RING, cols], w_raw[:, c % RAW_RING, cols],
                                        w_high[:, c % SPLIT_RING, cols].bitcast(F32),
                                        ALU.subtract).then_inc(w_low_vector, 1)

            def make_hot(q):
                r = hot_number(q) % HOT_RING
                hot_ring_left(dve, hot_number(q))
                dve.wait_ge(hot_loaded[r], 3 * 16 * (hot_number(q) // HOT_RING + 1))
                for k in range(HOT_TILES):
                    nc.vector.tensor_scalar(one_hot[r][0:HOT_P, k, :], hot_ids[0:HOT_P, r, :],
                                            hot_row[0:HOT_P, k:k + 1], None, ALU.is_equal)
                dve.wait_ge(hot_high_ready, hot_number(q) + 1)
                nc.vector.tensor_tensor(hot_split[r][0:HOT_P, :, D:2 * D],
                                        hot_table[0:HOT_P, r, :].rearrange("p (k d) -> p k d", d=D),
                                        hot_split[r][0:HOT_P, :, 0:D].bitcast(F32),
                                        ALU.subtract).then_inc(hot_ready, 1)

            dve.wait_ge(hot_rows_numbered, 1)
            nc.vector.tensor_copy(hot_row[:], hot_row_int[:]).then_inc(hot_rows_ready, 1)
            dve.wait_ge(identity_ready, 1)
            nc.vector.memset(halves_sum[:].bitcast(F32), 0.0).then_inc(halves_zeroed, 1)
            dve.wait_ge(halves_zeroed, 1)
            for q in range(2):
                half = slice(q * D, (q + 1) * D)
                nc.vector.tensor_copy(halves_sum[half, D:2 * D], identity[half, half]).then_inc(halves_ready, 1)
            dve.wait_ge(hot_rows_ready, 1)
            nc.vector.memset(selector[:], 0.0).then_inc(selector_zeroed, 1)
            dve.wait_ge(selector_zeroed, 1)
            for q in range(2):
                nc.vector.memset(selector[q * D:(q + 1) * D, QUAD - 2 + q:QUAD - 1 + q], 1.0).then_inc(selector_ready, 1)
            nc.vector.memset(z_sb[DENSE_ROW:P, Z_COUNT - 1, :], 0.0).then_inc(dense_zeroed, 1)

            steps = [s for s in low_steps if not by_gpsimd(s[2][0])]
            steps += hot_steps
            steps += [(transposes_at(m) + 0.6, "low", m) for m in gathered_couples]
            steps += [(SLOT_TILES * (s + 1), "multiply", s) for s in range(SLOTS)]
            for _, what, n in sorted(steps, key=lambda s: s[0]):
                if what == "split":
                    make_low(*n)
                elif what == "hot table":
                    make_hot(n)
                elif what == "low":
                    make_mover_low(n)
                else:
                    multiply(n)

        @block.tensor
        def _(pe):
            def fill_bank(k):
                _, kind, n = banked[k]
                if kind == "couple":
                    count = gather_number(n)
                    r = count % GATHER_RING
                    pe.wait_ge(gather_landed[r], 2 * BATCH_TILES * 16 * (count // GATHER_RING + 1))
                elif kind == "hot":
                    pe.wait_ge(hot_ready, hot_number(n) + 1)
                if k:
                    wait_bank_left(pe, k - 1)
                if kind == "couple":
                    for bt in range(BATCH_TILES):
                        last = nc.tensor.transpose(t_ps[:, bt * P:(bt + 1) * P], gathered[:, r, bt, :], identity[:])
                elif kind == "hot":
                    r = hot_number(n) % HOT_RING
                    for j in range(HOT_TILES):
                        last = nc.tensor.matmul(t_ps[:, :], hot_split[r][0:HOT_P, j, :], one_hot[r][0:HOT_P, j, :],
                                                start=(j == 0), stop=(j == HOT_TILES - 1))
                else:
                    for q in range(2):
                        last = nc.tensor.matmul(t_ps[:, :], halves_sum[:, D - q * D:D - q * D + P],
                                                mover[:, 2 * n + q, :], start=(q == 0), stop=(q == 1))
                last.then_inc(bank_filled, 1)

            def multiply(t):
                m = couple_of(t)
                i = t - m * m
                c, n = divmod(t, CHUNK_TILES)
                s, k = divmod(t, SLOT_TILES)
                if n == 0:
                    pe.wait_ge(w_high_ready, c + 1)
                    wait_low(pe, c)
                if i == 2 * m and m not in HOT_COUPLES:
                    pe.wait_ge(low_ready, gather_number(m) + 1)
                if k == 0 and s >= U_RING:
                    pe.wait_ge(prod_ready, s - U_RING + 1)
                out = u_ps[:, SLOT_TILES * (s % U_RING) + k, :]
                cols = slice(n * P, (n + 1) * P)
                nc.tensor.matmul(out, w_high[:, c % SPLIT_RING, cols], mover[:, i, :], start=True, stop=False)
                last = nc.tensor.matmul(out, w_low[:, c % SPLIT_RING, cols], mover[:, i, :], start=False, stop=True)
                if k == SLOT_TILES - 1:
                    last.then_inc(u_ready, 1)

            def sum_group(g):
                pe.wait_ge(prod_ready, GROUP_SLOTS * (g + 1))
                for t in range(GROUP_TILES * g, GROUP_TILES * (g + 1)):
                    k, q, r = z_place(t)
                    if t % Z_TILES == 0 and k >= Z_RING:
                        pe.wait_ge(z_ready, k - Z_RING + 1)
                    final = r == z_rows[k, q] - 1
                    at = QUAD - 2 - 2 * r
                    last = nc.tensor.matmul(z_ps[QUAD * q:QUAD * (q + 1), k % Z_RING, :],
                                            selector[:, at:at + QUAD],
                                            prod[:, t // SLOT_TILES % PROD_RING, t % SLOT_TILES, :],
                                            start=(r == 0), stop=final)
                last.then_inc(sums_ready, 1)

            def layer1(k, n):
                return nc.tensor.matmul(h1_ps[n], w1_sb[:, k, n * P:(n + 1) * P], z_sb[:, k, :],
                                        start=(k == 0), stop=(k == Z_COUNT - 1))

            z_rows = {}
            for t in range(TILES):
                k, q, r = z_place(t)
                z_rows[k, q] = r + 1
            pe.wait_ge(identity_ready, 1)
            pe.wait_ge(selector_ready, 2)
            pe.wait_ge(halves_ready, 2)
            next_group = 0
            next_step = 0
            for t in range(TILES):
                while next_step < len(banked) and banked[next_step][0] <= t:
                    fill_bank(next_step)
                    next_step += 1
                multiply(t)
                while ((t + 1) % GROUP_TILES == 0 and (t + 1) // SLOT_TILES >= GROUP_SLOTS * next_group + SUM_LAG
                       + GROUP_SLOTS * (next_group % Z_GROUPS == 0)):
                    sum_group(next_group)
                    next_group += 1

            pe.wait_ge(mlp_loaded, 5 * 16)
            wait_bank_left(pe, len(banked) - 1)
            pe.wait_ge(z_ready, Z_COUNT - 1)
            for n in range(H1_TILES):
                if left_at[n]:
                    pe.wait_ge(prod_ready, left_at[n])
                for k in range(Z_COUNT - 1):
                    layer1(k, n)
                while next_group < GROUPS and GROUP_SLOTS * (next_group + 1) <= left_at[n] + 1:
                    sum_group(next_group)
                    next_group += 1
            pe.wait_ge(dense_loaded, 16)
            pe.wait_ge(z_ready, Z_COUNT)
            for n in range(H1_TILES):
                layer1(Z_COUNT - 1, n).then_inc(h1_summed, 1)
            for k in range(H1_TILES):
                pe.wait_ge(h1_ready, k + 1)
                for n in range(H2_TILES):
                    last = nc.tensor.matmul(h2_ps[n], w2_sb[:, k, n * P:(n + 1) * P], h1_sb[:, k, :],
                                            start=(k == 0), stop=(k == H1_TILES - 1))
                    if k == H1_TILES - 1:
                        last.then_inc(h2_summed, 1)
            for k in range(H2_TILES):
                pe.wait_ge(h2_ready, k + 1)
                last = nc.tensor.matmul(y_ps, w3_sb[:, k:k + 1], h2_sb[:, k, :],
                                        start=(k == 0), stop=(k == H2_TILES - 1))
            last.then_inc(y_summed, 1)


def pair_index(i, j):
    return i * FIELDS - i * (i + 1) // 2 + j - i - 1


def kernel(**inputs):
    import concourse.bacc as bacc
    from concourse.bass_utils import run_bass_kernel_spmd

    small = [f for f in range(FIELDS) if inputs[f"tbl_{f}"].shape[0] == HOT_ROWS][:2 * len(HOT_COUPLES)]
    others = [f for f in range(FIELDS) if f not in small]
    order = [(small if q // 2 in HOT_COUPLES else others).pop(0) for q in range(FIELDS)]
    w = np.asarray(inputs["L0_rec_W"])
    w_tiles = np.zeros((TILES, 2, D, D), w.dtype)
    w1 = np.asarray(inputs["W_top1"])
    w1_rows = np.zeros((Z_COUNT, P, H1), w1.dtype)
    for t in range(TILES):
        m = couple_of(t)
        i = t - m * m
        k, q, r = z_place(t)
        for side in range(2):
            j = 2 * m + side
            if i < j:
                a, b = order[i], order[j]
                p = pair_index(min(a, b), max(a, b))
                w_tiles[t, side] = w[p] if a < b else w[p].T
                w1_rows[k, QUAD * q + 2 * r + side] = w1[p]
    w1_rows[Z_COUNT - 1, DENSE_ROW:DENSE_ROW + DENSE] = w1[-DENSE:]
    w_pairs = w_tiles.reshape(CHUNKS, CHUNK_TILES, 2, D, D).transpose(0, 3, 1, 2, 4).reshape(CHUNKS, D, CHUNK_COLS)

    arrays = {
        "dense_t": np.asarray(inputs["dense_ctx"]).T,
        "ids": np.asarray(inputs["ids"])[:, order],
        "ids_t": np.asarray(inputs["ids"])[:, order].T,
        "w_pairs": w_pairs,
        "w1": w1_rows,
        "b1": np.asarray(inputs["b_top1"]).reshape(H1_TILES, P).T,
        "w2": np.asarray(inputs["W_top2"]),
        "b2": np.asarray(inputs["b_top2"]).reshape(H2_TILES, P).T,
        "w3": np.asarray(inputs["W_top3"]).reshape(H2_TILES, P).T,
    }
    for f in range(FIELDS):
        arrays[f"tbl_{f}"] = np.asarray(inputs[f"tbl_{f}"])
    arrays = {f"in_{name}": np.ascontiguousarray(a) for name, a in arrays.items()}

    nc = bacc.Bacc("TRN2", target_bir_lowering=False, num_devices=1)
    ap = {
        name[3:]: nc.dram_tensor(name, a.shape, mybir.dt.from_np(a.dtype), kind="ExternalInput").ap()
        for name, a in arrays.items()
    }
    y = nc.dram_tensor("out_y", (BATCH, 1), F32, kind="ExternalOutput").ap()
    tower(nc, ap["dense_t"], ap["ids"], ap["ids_t"], [ap[f"tbl_{f}"] for f in order], ap["w_pairs"],
          ap["w1"], ap["b1"], ap["w2"], ap["b2"], ap["w3"], y)
    result = run_bass_kernel_spmd(nc, [arrays], core_ids=[0])
    return result.results[0]["out_y"]
```

```python
from contextlib import ExitStack

import numpy as np

import concourse.bass as bass
from concourse import mybir

P = 128
FIELDS = 40
D = 64
BATCH = 512
COUPLES = FIELDS // 2
DENSE = 16

HOT_COUPLES = (0, 2)
HOT_ROWS = 1000
HOT_TILES = 8
HOT_P = HOT_ROWS // HOT_TILES
HOT_LEAD = 16

OCTET_COUPLES = tuple(m for m in range(COUPLES) if m not in HOT_COUPLES)[:4]
OCTET_FIELDS = tuple(q for m in OCTET_COUPLES for q in (2 * m, 2 * m + 1))
OCTET = len(OCTET_FIELDS)
LATER = OCTET_COUPLES[-1] + 1
UNITS = FIELDS - 2 * LATER
UNIT_COLS = OCTET * D
MOVERS = FIELDS - OCTET



def couple_movers(m):
    if m < LATER:
        return list(range(2 * m + 1))
    return [q for q in range(2 * m + 1) if q not in OCTET_FIELDS]


TILE_LIST = [(m, i) for m in range(COUPLES) for i in couple_movers(m)]
TILES = len(TILE_LIST)
SLOT_TILES = 2
GROUP_TILES = 4
GROUPS = TILES // GROUP_TILES
GROUP_SLOTS = GROUP_TILES // SLOT_TILES
BLOCKS = GROUPS + UNITS
SLOTS = BLOCKS * GROUP_SLOTS
CHUNK_TILES = 8
CHUNKS = BLOCKS * GROUP_TILES // CHUNK_TILES
CHUNK_COLS = CHUNK_TILES * P
Z_TILES = 64
Z_SUMMED = -(-TILES // Z_TILES)
Z_GROUPS = Z_TILES // GROUP_TILES
UNIT_SUMS = UNITS * OCTET + DENSE
Z_TURNED = 2
Z_TURNED_ROWS = UNIT_SUMS // Z_TURNED
Z_COUNT = Z_SUMMED + Z_TURNED
QUAD = 32

H1, H2 = 512, 256
H1_TILES, H2_TILES = H1 // P, H2 // P
BATCH_TILES = BATCH // P

GATHER_RING = 3
PARTNER_RING = 4
RAW_RING = 3
SPLIT_RING = 4
U_RING = 3
PROD_RING = 5
UNIT_PROD_RING = 4
Z_RING = 1
HOT_RING = 2

SUM_LAG = 4
LEAD_TILES = 4
LEAD_FROM = 9
GATHER_AHEAD = 1
SPLIT_LEAD = 18
MOVER_LOW_FROM = 14
MOVER_LOW_EVERY = 1
LOW_LATE = 2
LOW_PARTS = 1
GPSIMD_FROM = 10
GPSIMD_EVERY = 1

UNIT_FROM = 24
UNIT_TO = 132
UNIT_POWER = 0.9
UNIT_SIDE = 1
POOL_FROM = 1
POOL_EVERY = 8
VECTOR_EVERY = 2
SUM_DELAY = 10
SUM_STEP = 2
STAGES = ((1, 8), (2, 4), (3, 3))
Z_DELAY = 6
TURN_DELAY = 12

F32 = mybir.dt.float32
F32R = mybir.dt.float32r
I32 = mybir.dt.int32
ALU = mybir.AluOpType
ACT = mybir.ActivationFunctionType


def tile_start(m):
    return sum(x < m for x, _ in TILE_LIST)


def unit_couple(j):
    return LATER + j // 2


def slot_list():
    slots = []
    k = 0
    for n in range(GROUPS * GROUP_SLOTS):
        slots.append(("tiles", n))
        while (k < UNITS * GROUP_SLOTS and n % GROUP_SLOTS == UNIT_SIDE
               and tile_start(unit_couple(k // GROUP_SLOTS)) < SLOT_TILES * (n + 1)
               and n + 1 >= UNIT_FROM + (UNIT_TO - UNIT_FROM) * (k / (UNITS * GROUP_SLOTS)) ** UNIT_POWER and n + 1 < GROUP_SLOTS * (GROUPS - 1)):
            slots.append(("unit", k))
            k += 1
    assert k == UNITS * GROUP_SLOTS
    return slots


SLOT_LIST = slot_list()
SUM_SLOTS = [s for s in range(SLOTS) if SLOT_LIST[s][0] == "tiles"]
UNIT_SLOTS = [s for s in range(SLOTS) if SLOT_LIST[s][0] == "unit"]
BLOCK_LIST = list(dict.fromkeys((what, n // GROUP_SLOTS) for what, n in SLOT_LIST))
SLOT_BLOCK = [BLOCK_LIST.index((what, n // GROUP_SLOTS)) for what, n in SLOT_LIST]
SLOT_CHUNK = [b * GROUP_TILES // CHUNK_TILES for b in SLOT_BLOCK]


def slots_through_group(g):
    return SUM_SLOTS[GROUP_SLOTS * (g + 1) - 1] + 1


def place(t):
    return SLOT_TILES * SUM_SLOTS[t // SLOT_TILES] + t % SLOT_TILES


def summed_by(k):
    if k >= POOL_FROM and (k - POOL_FROM) % POOL_EVERY == 0:
        return "gpsimd"
    return "vector" if k % VECTOR_EVERY == VECTOR_EVERY - 1 else "scalar"


def slots_summed(k, *engines):
    return sum(summed_by(x) in engines for x in range(k))


def unit_entry(k):
    return slots_summed(k, "scalar", "gpsimd")


def z_place(t):
    k, n = divmod(t, Z_TILES)
    return k, n % GROUP_TILES, n // GROUP_TILES


def mover_slot(q):
    return q if q < MOVERS else OCTET_FIELDS[q - MOVERS]


def hot_number(q):
    return 2 * HOT_COUPLES.index(q // 2) + q % 2


def gather_number(m):
    return sum(x not in HOT_COUPLES for x in range(m))


def ring_number(m):
    return gather_number(m) - len(OCTET_COUPLES)


def by_gpsimd(c):
    return c >= GPSIMD_FROM and (c - GPSIMD_FROM) % GPSIMD_EVERY == 0


def mover_by_gpsimd(m):
    return m >= MOVER_LOW_FROM and (m - MOVER_LOW_FROM) % MOVER_LOW_EVERY == 0


def low_count(c):
    return sum(by_gpsimd(x) == by_gpsimd(c) for x in range(c + 1))


def transposes_at(m):
    lead = LEAD_TILES if m >= LEAD_FROM else 0
    return max(place(tile_start(m - 1)) if m else 0, place(tile_start(m)) - lead)


def z_at(k):
    return SLOT_TILES * (slots_through_group(Z_GROUPS * (k + 1) - 1) + SUM_LAG - GROUP_SLOTS)


def stage_tiles(stage):
    first = STAGES[stage - 1][0] + 1 if stage else 0
    return list(range(first, STAGES[stage][0] + 1)) + ([Z_SUMMED] if stage == len(STAGES) - 1 else [])


def turn_at(h):
    columns = min(Z_TURNED_ROWS * (h + 1), UNITS * OCTET)
    last = UNIT_SLOTS[GROUP_SLOTS * (-(-columns // OCTET)) - 1]
    return min(SLOT_TILES * (last + 1) + TURN_DELAY, SLOT_TILES * SLOTS)


def bank_steps():
    steps = []
    for m in range(COUPLES):
        at = transposes_at(m)
        if m in HOT_COUPLES:
            steps += [(at - 2, "hot", 2 * m), (at - 1, "hot", 2 * m + 1), (at - 0.5, "pair", m)]
        else:
            steps.append((at, "couple", m))
    steps += [(turn_at(h), "turn", h) for h in range(Z_TURNED)]
    for stage, (last, step) in enumerate(STAGES):
        steps += [(z_at(last) + Z_DELAY + step * n, "h1 part", (stage, n)) for n in range(H1_TILES)]
    return sorted(steps, key=lambda s: s[0])


def tower(nc, dense, ids, ids_t, tables, w_pairs, w1, b1, w2, b2, w3, y):
    with ExitStack() as ctx:
        def sb(name, shape, dt=F32):
            return ctx.enter_context(nc.sbuf_tensor(name, shape, dt))

        def ps(name, shape):
            return ctx.enter_context(nc.psum_tensor(name, shape, F32))

        def sem(name):
            return ctx.enter_context(nc.semaphore(name))

        ids_sb = sb("ids_sb", [P, BATCH_TILES, FIELDS], I32)
        octet = sb("octet", [P, BATCH_TILES, UNIT_COLS])
        gathered = sb("gathered", [P, GATHER_RING, BATCH_TILES, 2 * D])
        partner = sb("partner", [P, PARTNER_RING, BATCH])
        mover = sb("mover", [P, MOVERS, BATCH], F32R)
        w_raw = sb("w_raw", [P, RAW_RING, CHUNK_COLS])
        w_high = sb("w_high", [P, SPLIT_RING, CHUNK_COLS], F32R)
        w_low = sb("w_low", [P, SPLIT_RING, CHUNK_COLS], F32R)
        prod = sb("prod", [P, PROD_RING, SLOT_TILES, BATCH])
        h1_part = sb("h1_part", [P, H1_TILES, BATCH])
        unit_prod = sb("unit_prod", [P, UNIT_PROD_RING, SLOT_TILES, UNIT_COLS])
        unit_sums = sb("unit_sums", [P, BATCH_TILES, UNIT_SUMS])
        z_sb = sb("z_sb", [P, Z_COUNT, BATCH])
        w1_sb = sb("w1_sb", [P, Z_COUNT, H1])
        w2_sb = gathered[:].rearrange("p r t c -> p (r t c)")[:, 0:H1_TILES * H2].rearrange("p (k n) -> p k n", n=H2)
        w3_sb = sb("w3_sb", [P, H2_TILES])
        b1_sb = sb("b1_sb", [P, H1_TILES])
        b2_sb = sb("b2_sb", [P, H2_TILES])
        hidden = w_raw[:].rearrange("p r c -> p (r c)").rearrange("p (n b) -> p n b", b=BATCH)
        h1_sb = hidden[:, 0:H1_TILES, :]
        h2_sb = hidden[:, H1_TILES:H1_TILES + H2_TILES, :]
        y_sb = partner[0:1, 0, :]
        hot_row = sb("hot_row", [P, HOT_TILES])
        hot_row_int = sb("hot_row_int", [P, HOT_TILES], I32)
        hot_table = z_sb[:, 0:HOT_RING, :]
        hot_ids = z_sb[:, HOT_RING:2 * HOT_RING, :].bitcast(I32)
        top = MOVERS
        one_hot = [mover[:, top - HOT_TILES * (r + 1):top - HOT_TILES * r, :] for r in range(HOT_RING)]
        top -= HOT_TILES * HOT_RING
        hot_split = [mover[:, top - 2 * (r + 1):top - 2 * r, :].rearrange("p a (k c) -> p (a k) c", c=2 * D)
                     for r in range(HOT_RING)]
        top -= 2 * HOT_RING
        halves_sum = mover[:, top - 1, 0:3 * D]
        identity = sb("identity", [P, P])
        selector = sb("selector", [P, 2 * QUAD - 2])

        u_ps = ps("u_ps", [P, U_RING * SLOT_TILES, BATCH])
        z_ps = ps("z_ps", [P, Z_RING, BATCH])
        t_ps = ps("t_ps", [P, BATCH])

        tail = [(s, u_ps[:, SLOT_TILES * (s % U_RING) + k, :]) for s in range(SLOTS - U_RING, SLOTS)
                for k in range(SLOT_TILES)]
        h1_ps = [bank for _, bank in tail[:3]] + [t_ps[:, :]]
        left_at = [s + 1 for s, _ in tail[:3]] + [0]
        h2_ps = [tail[3][1], tail[4][1]]
        y_ps = tail[5][1][0:1, :]

        ids_loaded = sem("ids_loaded")
        mlp_loaded = sem("mlp_loaded")
        w2_loaded = sem("w2_loaded")
        dense_loaded = sem("dense_loaded")
        octet_landed = [sem(f"octet_landed{k}") for k in range(len(OCTET_COUPLES))]
        gather_landed = [sem(f"gather_landed{r}") for r in range(GATHER_RING)]
        w_loaded = [sem(f"w_loaded{r}") for r in range(RAW_RING)]
        identity_zeroed = sem("identity_zeroed")
        identity_ready = sem("identity_ready")
        selector_zeroed = sem("selector_zeroed")
        selector_ready = sem("selector_ready")
        bank_filled = sem("bank_filled")
        bank_left = sem("bank_left")
        hot_loaded = [sem(f"hot_loaded{r}") for r in range(HOT_RING)]
        hot_rows_numbered = sem("hot_rows_numbered")
        hot_rows_ready = sem("hot_rows_ready")
        hot_high_ready = sem("hot_high_ready")
        hot_ready = sem("hot_ready")
        halves_zeroed = sem("halves_zeroed")
        halves_ready = sem("halves_ready")
        partner_ready = sem("partner_ready")
        low_vector = sem("low_vector")
        first_low_gpsimd = sem("first_low_gpsimd")
        low_gpsimd = sem("low_gpsimd")
        w_high_ready = sem("w_high_ready")
        w_low_vector = sem("w_low_vector")
        w_low_gpsimd = sem("w_low_gpsimd")
        u_ready = sem("u_ready")
        prod_ready = sem("prod_ready")
        unit_sums_gpsimd = sem("unit_sums_gpsimd")
        halved = sem("halved")
        unit_sums_scalar = sem("unit_sums_scalar")
        sums_ready = sem("sums_ready")
        z_ready = sem("z_ready")
        h1_summed = sem("h1_summed")
        h1_ready = sem("h1_ready")
        h1_part_ready = sem("h1_part_ready")
        h1_whole = sem("h1_whole")
        h2_summed = sem("h2_summed")
        h2_ready = sem("h2_ready")
        y_summed = sem("y_summed")
        y_ready = sem("y_ready")
        y_stored = sem("y_stored")

        block = ctx.enter_context(nc.Block())

        def wait_mover_low(eng, m):
            eng.wait_ge(low_gpsimd if mover_by_gpsimd(m) else low_vector,
                        sum(mover_by_gpsimd(x) == mover_by_gpsimd(m) for x in gathered_couples if x <= m))

        def wait_low(eng, c):
            eng.wait_ge(w_low_gpsimd if by_gpsimd(c) else w_low_vector, LOW_PARTS * low_count(c))

        def wait_unit_summed(eng, k):
            if summed_by(k) == "scalar":
                eng.wait_ge(unit_sums_scalar, SLOT_TILES * slots_summed(k + 1, "scalar"))
            elif summed_by(k) == "gpsimd":
                eng.wait_ge(unit_sums_gpsimd, slots_summed(k + 1, "gpsimd"))
            else:
                eng.wait_ge(prod_ready, UNIT_SLOTS[k] + 1)

        gathered_couples = [m for m in range(COUPLES) if m not in HOT_COUPLES]
        banked = bank_steps()
        bank_number = {(kind, n): k for k, (_, kind, n) in enumerate(banked)}

        def by_vector(kind, n):
            return kind == "h1 part" and n[0] > 0

        def wait_bank_left(eng, k):
            _, kind, n = banked[k]
            if kind == "pair":
                eng.wait_ge(partner_ready, n + 1)
            elif by_vector(kind, n):
                eng.wait_ge(h1_part_ready, sum(by_vector(*x[1:]) for x in banked[:k + 1]))
            else:
                eng.wait_ge(bank_left, sum(x[1] != "pair" and not by_vector(*x[1:]) for x in banked[:k + 1]))

        def hot_ring_left(eng, n):
            if n >= HOT_RING:
                q = 2 * HOT_COUPLES[(n - HOT_RING) // 2] + n % 2
                eng.wait_ge(bank_filled, bank_number["hot", q] + 1)

        def slots_through_couple(m):
            return SUM_SLOTS[(tile_start(m + 1) - 1) // SLOT_TILES] + 1

        def chunk_used(c):
            return max(s for s in range(SLOTS) if SLOT_CHUNK[s] == c) + 1

        def chunk_at(c):
            at = SLOT_TILES * SLOT_CHUNK.index(c) - SPLIT_LEAD
            return max(at, SLOT_TILES * chunk_used(c - SPLIT_RING) + 0.2) if c >= SPLIT_RING else at

        split_steps = [(chunk_at(c), "split", c) for c in range(CHUNKS)]
        hot_steps = []
        for m in HOT_COUPLES:
            for q in (2 * m, 2 * m + 1):
                at = banked[bank_number["hot", q]][0] - HOT_LEAD
                if hot_number(q) >= HOT_RING:
                    last = hot_number(q) - HOT_RING
                    at = max(at, banked[bank_number["hot", 2 * HOT_COUPLES[last // 2] + last % 2]][0] + 0.1)
                hot_steps.append((at, "hot table", q))
        low_steps = [(chunk_at(c) + LOW_LATE * (part + 1), "split", (c, part))
                     for c in range(CHUNKS) for part in range(LOW_PARTS)]

        @block.sync
        def _(sp):
            def load_hot(q):
                n = hot_number(q)
                if n >= HOT_RING:
                    sp.wait_ge(hot_ready, n - HOT_RING + 1)
                r = n % HOT_RING
                rows = tables[q].rearrange("(p k) d -> p (k d)", k=HOT_TILES)
                for a, b in ((0, 112), (112, HOT_P)):
                    sp.dma_start(hot_table[a:b, r, :], rows[a:b, :]).then_inc(hot_loaded[r], 16)
                sp.dma_start(hot_ids[:, r, :], ids_t[q:q + 1, :].to_broadcast([P, BATCH])).then_inc(hot_loaded[r], 16)

            sp.dma_start(ids_sb[:], ids.rearrange("(t p) f -> p t f", p=P)).then_inc(ids_loaded, 16)
            hot_fields = [q for _, _, q in hot_steps]
            for q in hot_fields[:HOT_RING]:
                load_hot(q)
            for c in range(CHUNKS):
                if c >= RAW_RING:
                    sp.wait_ge(w_high_ready, c - RAW_RING + 1)
                    wait_low(sp, c - RAW_RING)
                for half in range(2):
                    sp.dma_start(w_raw[half * D:(half + 1) * D, c % RAW_RING, :],
                                 w_pairs[c]).then_inc(w_loaded[c % RAW_RING], 16)
                if c == RAW_RING - 1:
                    for q in hot_fields[HOT_RING:]:
                        load_hot(q)
                if c == RAW_RING + len(hot_fields):
                    sp.dma_start(w1_sb[:], w1.rearrange("k p n -> p k n")).then_inc(mlp_loaded, 16)
                    sp.dma_start(w3_sb[:], w3).then_inc(mlp_loaded, 16)
                    sp.dma_start(b1_sb[:], b1).then_inc(mlp_loaded, 16)
                    sp.dma_start(b2_sb[:], b2).then_inc(mlp_loaded, 16)
                    sp.dma_start(unit_sums[:, :, UNITS * OCTET:], dense.rearrange("(t p) c -> p t c", p=P)).then_inc(dense_loaded, 16)
            sp.wait_ge(bank_filled, bank_number["couple", COUPLES - 1] + 1)
            sp.dma_start(w2_sb, w2.rearrange("(k p) n -> p k n", p=P)).then_inc(w2_loaded, 16)
            sp.wait_ge(y_ready, 1)
            sp.dma_start(y.rearrange("b o -> o b"), y_sb).then_inc(y_stored, 16)
            sp.wait_ge(y_stored, 16)

        @block.gpsimd
        def _(pool):
            def gather(m):
                n, r = divmod(ring_number(m), GATHER_RING)
                if n > 0:
                    last = gathered_couples[gather_number(m) - GATHER_RING]
                    pool.wait_ge(bank_filled, bank_number["couple", last] + 1)
                for side in range(2):
                    for bt in range(BATCH_TILES):
                        q = 2 * m + side
                        if m in OCTET_COUPLES:
                            at = OCTET_FIELDS.index(q) * D
                            to, landed = octet[:, bt, at:at + D], octet_landed[gather_number(m)]
                        else:
                            to, landed = gathered[:, r, bt, side * D:(side + 1) * D], gather_landed[r]
                        nc.gpsimd.indirect_dma_start(
                            out=to,
                            out_offset=None,
                            in_=tables[q],
                            in_offset=bass.IndirectOffsetOnAxis(ap=ids_sb[:, bt, q:q + 1], axis=0),
                        ).then_inc(landed, 16)

            def make_mover_low(m):
                wait_bank_left(pool, bank_number["couple", m])
                raw = partner[:, m % PARTNER_RING, :]
                for done, count in ((w_low_gpsimd, lows_made), (unit_sums_gpsimd, units_summed)):
                    if count:
                        pool.wait_ge(done, count)
                for r in range(min(GATHER_RING, gathers_made)):
                    turns = (gathers_made - 1 - r) // GATHER_RING + 1
                    pool.wait_ge(gather_landed[r], 2 * BATCH_TILES * 16 * turns)
                nc.gpsimd.tensor_tensor(mover[D:P, mover_slot(2 * m), :], raw[0:D, :],
                                        mover[0:D, mover_slot(2 * m), :].bitcast(F32),
                                        ALU.subtract).then_inc(first_low_gpsimd, 1)
                pool.wait_ge(first_low_gpsimd, movers_made + 1)
                nc.gpsimd.tensor_tensor(mover[0:D, mover_slot(2 * m + 1), :], raw[D:P, :],
                                        mover[D:P, mover_slot(2 * m + 1), :].bitcast(F32),
                                        ALU.subtract).then_inc(low_gpsimd, 1)
                pool.wait_ge(low_gpsimd, movers_made + 1)

            def make_low(c, part):
                pool.wait_ge(w_high_ready, c + 1)
                cols = slice(part * CHUNK_COLS // LOW_PARTS, (part + 1) * CHUNK_COLS // LOW_PARTS)
                nc.gpsimd.tensor_tensor(w_low[:, c % SPLIT_RING, cols], w_raw[:, c % RAW_RING, cols],
                                        w_high[:, c % SPLIT_RING, cols].bitcast(F32),
                                        ALU.subtract).then_inc(w_low_gpsimd, 1)

            def sum_unit(k):
                pool.wait_ge(prod_ready, UNIT_SLOTS[k] + 1)
                j, bt = k // GROUP_SLOTS, k % GROUP_SLOTS * SLOT_TILES
                entry = unit_prod[:, unit_entry(k) % UNIT_PROD_RING, :, :]
                values = entry.rearrange("p s (f e) -> p (s f) e", e=D)
                done = (D.bit_length() - 2) * slots_summed(k, "gpsimd")
                half = D // 2
                while half > 1:
                    nc.gpsimd.tensor_tensor(values[:, :, 0:half], values[:, :, 0:half], values[:, :, half:2 * half],
                                            ALU.add).then_inc(halved, 1)
                    done += 1
                    pool.wait_ge(halved, done)
                    half //= 2
                values = entry.rearrange("p s (f e) -> p s f e", e=D)
                nc.gpsimd.tensor_tensor(unit_sums[:, bt:bt + SLOT_TILES, OCTET * j:OCTET * (j + 1)],
                                        values[:, :, :, 0], values[:, :, :, 1], ALU.add).then_inc(unit_sums_gpsimd, 1)

            nc.gpsimd.memset(identity[:], 0.0).then_inc(identity_zeroed, 1)
            pool.wait_ge(identity_zeroed, 1)
            nc.gpsimd.affine_select(out=identity[:], in_=identity[:], compare_op=ALU.not_equal, fill=1.0,
                                    base=0, pattern=[[-1, P]], channel_multiplier=1).then_inc(identity_ready, 1)
            nc.gpsimd.iota(hot_row_int[:], pattern=[[1, HOT_TILES]], base=0,
                           channel_multiplier=HOT_TILES).then_inc(hot_rows_numbered, 1)
            pool.wait_ge(ids_loaded, 16)
            steps = [(transposes_at(max(m - GATHER_AHEAD, 0)) - 1, "gather", m) for m in gathered_couples]
            steps += [s for s in low_steps if by_gpsimd(s[2][0])]
            steps += [(transposes_at(m) + 0.6, "low", m) for m in gathered_couples if mover_by_gpsimd(m)]
            steps += [(SLOT_TILES * (UNIT_SLOTS[k] + 1) + SUM_DELAY, "unit", k)
                      for k in range(len(UNIT_SLOTS)) if summed_by(k) == "gpsimd"]
            lows_made = units_summed = movers_made = gathers_made = 0
            for _, what, n in sorted(steps, key=lambda s: s[0]):
                if what == "gather":
                    gather(n)
                    gathers_made += n not in OCTET_COUPLES
                elif what == "unit":
                    sum_unit(n)
                    units_summed += 1
                elif what == "low":
                    make_mover_low(n)
                    movers_made += 1
                else:
                    make_low(*n)
                    lows_made += 1

        @block.scalar
        def _(act):
            def make_high(c):
                act.wait_ge(w_loaded[c % RAW_RING], 32 * (c // RAW_RING + 1))
                if c >= SPLIT_RING:
                    act.wait_ge(u_ready, chunk_used(c - SPLIT_RING))
                nc.scalar.copy(w_high[:, c % SPLIT_RING, :], w_raw[:, c % RAW_RING, :]).then_inc(w_high_ready, 1)

            def make_hot_high(q):
                r = hot_number(q) % HOT_RING
                act.wait_ge(hot_loaded[r], 3 * 16 * (hot_number(q) // HOT_RING + 1))
                hot_ring_left(act, hot_number(q))
                nc.scalar.copy(hot_split[r][0:HOT_P, :, 0:D],
                               hot_table[0:HOT_P, r, :].rearrange("p (k d) -> p k d", d=D)).then_inc(hot_high_ready, 1)

            def take_hot(q):
                act.wait_ge(bank_filled, bank_number["hot", q] + 1)
                nc.scalar.copy(mover[:, mover_slot(q), :], t_ps[:, :]).then_inc(bank_left, 1)

            def take_partner(m):
                if m >= PARTNER_RING:
                    last = m - PARTNER_RING
                    act.wait_ge(prod_ready, slots_through_couple(last))
                    if last not in HOT_COUPLES:
                        wait_mover_low(act, last)
                return nc.scalar.copy(partner[:, m % PARTNER_RING, :], t_ps[:, :]).then_inc(partner_ready, 1)

            def take_pair(m):
                act.wait_ge(bank_filled, bank_number["pair", m] + 1)
                take_partner(m)

            def take_couple(m):
                act.wait_ge(bank_filled, bank_number["couple", m] + 1)
                take_partner(m)
                nc.scalar.copy(mover[0:D, mover_slot(2 * m), :], t_ps[0:D, :])
                nc.scalar.copy(mover[D:P, mover_slot(2 * m + 1), :], t_ps[D:P, :]).then_inc(bank_left, 1)

            def take_z(k):
                act.wait_ge(sums_ready, min(Z_GROUPS * (k + 1), GROUPS))
                nc.scalar.copy(z_sb[:, k, :], z_ps[:, k % Z_RING, :]).then_inc(z_ready, 1)

            def take_turned(h):
                act.wait_ge(bank_filled, bank_number["turn", h] + 1)
                nc.scalar.copy(z_sb[0:Z_TURNED_ROWS, Z_SUMMED + h, :], t_ps[0:Z_TURNED_ROWS, :]).then_inc(bank_left, 1)

            def take_part(n):
                act.wait_ge(mlp_loaded, 4 * 16)
                act.wait_ge(bank_filled, bank_number["h1 part", (0, n)] + 1)
                nc.scalar.activation(h1_part[:, n, :], t_ps[:, :], ACT.Identity,
                                     bias=b1_sb[:, n:n + 1]).then_inc(bank_left, 1)

            def sum_unit(k, side):
                act.wait_ge(prod_ready, UNIT_SLOTS[k] + 1)
                j, bt = k // GROUP_SLOTS, k % GROUP_SLOTS * SLOT_TILES + side
                for o in range(OCTET):
                    product = unit_prod[:, unit_entry(k) % UNIT_PROD_RING, side, o * D:(o + 1) * D]
                    last = nc.scalar.activation(product, product, ACT.Copy,
                                                accum_out=unit_sums[:, bt, OCTET * j + o:OCTET * j + o + 1])
                last.then_inc(unit_sums_scalar, 1)

            steps = split_steps + [s for s in banked if not by_vector(*s[1:])] + hot_steps
            steps += [(z_at(k), "z", k) for k in range(Z_SUMMED - 1)]
            scalar_units = [k for k in range(len(UNIT_SLOTS)) if summed_by(k) == "scalar"]
            steps += [(SLOT_TILES * (UNIT_SLOTS[k] + 1) + SUM_DELAY + SUM_STEP * side, "unit", (k, side))
                      for k in scalar_units for side in range(SLOT_TILES)]
            for _, what, n in sorted(steps, key=lambda s: s[0]):
                if what == "split":
                    make_high(n)
                elif what == "hot table":
                    make_hot_high(n)
                elif what == "hot":
                    take_hot(n)
                elif what == "pair":
                    take_pair(n)
                elif what == "couple":
                    take_couple(n)
                elif what == "turn":
                    take_turned(n)
                elif what == "h1 part":
                    take_part(n[1])
                elif what == "unit":
                    sum_unit(*n)
                else:
                    take_z(n)
            take_z(Z_SUMMED - 1)

            for n in range(H1_TILES):
                act.wait_ge(h1_whole, n + 1)
                nc.scalar.activation(h1_sb[:, n, :], h1_part[:, n, :], ACT.Relu).then_inc(h1_ready, 1)
            for n in range(H2_TILES):
                act.wait_ge(h2_summed, n + 1)
                nc.scalar.activation(h2_sb[:, n, :], h2_ps[n], ACT.Relu, bias=b2_sb[:, n:n + 1]).then_inc(h2_ready, 1)
            act.wait_ge(y_summed, 1)
            nc.scalar.copy(y_sb, y_ps).then_inc(y_ready, 1)

        @block.vector
        def _(dve):
            def multiply(s):
                n = SUM_SLOTS.index(s)
                first, last = (TILE_LIST[t][0] for t in (SLOT_TILES * n, SLOT_TILES * n + 1))
                dve.wait_ge(partner_ready, last + 1)
                dve.wait_ge(u_ready, s + 1)
                if n >= PROD_RING:
                    dve.wait_ge(sums_ready, (n - PROD_RING) // GROUP_SLOTS + 1)
                r = first % PARTNER_RING
                if first == last:
                    by = partner[:, r, :].unsqueeze(1).to_broadcast([P, SLOT_TILES, BATCH])
                else:
                    by = partner[:, r:r + 2, :]
                u = SLOT_TILES * (s % U_RING)
                nc.vector.tensor_tensor(prod[:, n % PROD_RING, :, :], u_ps[:, u:u + SLOT_TILES, :], by,
                                        ALU.mult).then_inc(prod_ready, 1)

            def multiply_unit(k):
                s = UNIT_SLOTS[k]
                dve.wait_ge(u_ready, s + 1)
                u = SLOT_TILES * (s % U_RING)
                j, bt = k // GROUP_SLOTS, k % GROUP_SLOTS * SLOT_TILES
                if summed_by(k) != "vector":
                    n = unit_entry(k)
                    if n >= UNIT_PROD_RING:
                        wait_unit_summed(dve, max(x for x in range(k) if unit_entry(x) == n - UNIT_PROD_RING
                                                  and summed_by(x) != "vector"))
                    nc.vector.tensor_tensor(unit_prod[:, n % UNIT_PROD_RING, :, :], u_ps[:, u:u + SLOT_TILES, :],
                                            octet[:, bt:bt + SLOT_TILES, :], ALU.mult).then_inc(prod_ready, 1)
                    return
                for side in range(SLOT_TILES):
                    for o in range(OCTET):
                        product = u_ps[:, u + side, o * D:(o + 1) * D]
                        last = nc.vector.scalar_tensor_tensor(
                            product, product, 1.0, octet[:, bt + side, o * D:(o + 1) * D], ALU.mult, ALU.mult, accum_out=unit_sums[:, bt + side, OCTET * j + o:OCTET * j + o + 1])
                last.then_inc(prod_ready, 1)

            def make_mover_low(m):
                wait_bank_left(dve, bank_number["couple", m])
                raw = partner[:, m % PARTNER_RING, :]
                nc.vector.tensor_tensor(mover[D:P, mover_slot(2 * m), :], raw[0:D, :],
                                        mover[0:D, mover_slot(2 * m), :].bitcast(F32), ALU.subtract)
                nc.vector.tensor_tensor(mover[0:D, mover_slot(2 * m + 1), :], raw[D:P, :],
                                        mover[D:P, mover_slot(2 * m + 1), :].bitcast(F32), ALU.subtract).then_inc(low_vector, 1)

            def make_low(c, part):
                dve.wait_ge(w_high_ready, c + 1)
                cols = slice(part * CHUNK_COLS // LOW_PARTS, (part + 1) * CHUNK_COLS // LOW_PARTS)
                nc.vector.tensor_tensor(w_low[:, c % SPLIT_RING, cols], w_raw[:, c % RAW_RING, cols],
                                        w_high[:, c % SPLIT_RING, cols].bitcast(F32),
                                        ALU.subtract).then_inc(w_low_vector, 1)

            def add_part(stage, n):
                dve.wait_ge(bank_filled, bank_number["h1 part", (stage, n)] + 1)
                nc.vector.tensor_tensor(h1_part[:, n, :], t_ps[:, :], h1_part[:, n, :],
                                        ALU.add).then_inc(h1_part_ready, 1)

            def make_hot(q):
                r = hot_number(q) % HOT_RING
                hot_ring_left(dve, hot_number(q))
                dve.wait_ge(hot_loaded[r], 3 * 16 * (hot_number(q) // HOT_RING + 1))
                for k in range(HOT_TILES):
                    nc.vector.tensor_scalar(one_hot[r][0:HOT_P, k, :], hot_ids[0:HOT_P, r, :],
                                            hot_row[0:HOT_P, k:k + 1], None, ALU.is_equal)
                dve.wait_ge(hot_high_ready, hot_number(q) + 1)
                nc.vector.tensor_tensor(hot_split[r][0:HOT_P, :, D:2 * D],
                                        hot_table[0:HOT_P, r, :].rearrange("p (k d) -> p k d", d=D),
                                        hot_split[r][0:HOT_P, :, 0:D].bitcast(F32),
                                        ALU.subtract).then_inc(hot_ready, 1)

            dve.wait_ge(hot_rows_numbered, 1)
            nc.vector.tensor_copy(hot_row[:], hot_row_int[:]).then_inc(hot_rows_ready, 1)
            dve.wait_ge(identity_ready, 1)
            nc.vector.memset(halves_sum.bitcast(F32), 0.0).then_inc(halves_zeroed, 1)
            dve.wait_ge(halves_zeroed, 1)
            for q in range(2):
                half = slice(q * D, (q + 1) * D)
                nc.vector.tensor_copy(halves_sum[half, D:2 * D], identity[half, half]).then_inc(halves_ready, 1)
            dve.wait_ge(hot_rows_ready, 1)
            nc.vector.memset(selector[:], 0.0).then_inc(selector_zeroed, 1)
            dve.wait_ge(selector_zeroed, 1)
            for q in range(2):
                nc.vector.memset(selector[q * D:(q + 1) * D, QUAD - 2 + q:QUAD - 1 + q], 1.0).then_inc(selector_ready, 1)

            steps = [s for s in low_steps if not by_gpsimd(s[2][0])]
            steps += hot_steps
            steps += [(transposes_at(m) + 0.6, "low", m) for m in gathered_couples if not mover_by_gpsimd(m)]
            steps += [(at + 0.1, what, n) for at, what, n in banked if by_vector(what, n)]
            steps += [(SLOT_TILES * (s + 1), "multiply", s) for s in SUM_SLOTS]
            steps += [(SLOT_TILES * (s + 1), "unit", k) for k, s in enumerate(UNIT_SLOTS)]
            for _, what, n in sorted(steps, key=lambda s: s[0]):
                if what == "split":
                    make_low(*n)
                elif what == "hot table":
                    make_hot(n)
                elif what == "low":
                    make_mover_low(n)
                elif what == "unit":
                    multiply_unit(n)
                elif what == "h1 part":
                    add_part(*n)
                else:
                    multiply(n)
            for n in range(H1_TILES):
                dve.wait_ge(h1_summed, n + 1)
                nc.vector.tensor_tensor(h1_part[:, n, :], h1_ps[n], h1_part[:, n, :], ALU.add).then_inc(h1_whole, 1)

        @block.tensor
        def _(pe):
            def fill_bank(k):
                _, kind, n = banked[k]
                if kind == "couple":
                    if n in OCTET_COUPLES:
                        pe.wait_ge(octet_landed[gather_number(n)], 2 * BATCH_TILES * 16)
                    else:
                        turn, r = divmod(ring_number(n), GATHER_RING)
                        pe.wait_ge(gather_landed[r], 2 * BATCH_TILES * 16 * (turn + 1))
                elif kind == "hot":
                    pe.wait_ge(hot_ready, hot_number(n) + 1)
                elif kind == "turn":
                    slots = min(-(-Z_TURNED_ROWS * (n + 1) // OCTET), UNITS) * GROUP_SLOTS
                    for engine in ("scalar", "gpsimd", "vector"):
                        wait_unit_summed(pe, max(k for k in range(slots) if summed_by(k) == engine))
                    if n == Z_TURNED - 1:
                        pe.wait_ge(dense_loaded, 16)
                elif kind == "h1 part":
                    pe.wait_ge(mlp_loaded, 4 * 16)
                    pe.wait_ge(z_ready, STAGES[n[0]][0] + 1)
                    if Z_SUMMED in stage_tiles(n[0]):
                        wait_bank_left(pe, bank_number["turn", 0])
                if k:
                    wait_bank_left(pe, k - 1)
                if kind == "couple":
                    for bt in range(BATCH_TILES):
                        if n in OCTET_COUPLES:
                            at = OCTET_FIELDS.index(2 * n) * D
                            values = octet[:, bt, at:at + 2 * D]
                        else:
                            values = gathered[:, r, bt, :]
                        last = nc.tensor.transpose(t_ps[:, bt * P:(bt + 1) * P], values, identity[:])
                elif kind == "h1 part":
                    tiles = stage_tiles(n[0])
                    for z in tiles:
                        last = layer1(t_ps[:, :], z, n[1], z == tiles[0], z == tiles[-1])
                elif kind == "turn":
                    for bt in range(BATCH_TILES):
                        last = nc.tensor.transpose(t_ps[0:Z_TURNED_ROWS, bt * P:(bt + 1) * P],
                                                   unit_sums[:, bt, n * Z_TURNED_ROWS:(n + 1) * Z_TURNED_ROWS],
                                                   identity[:])
                elif kind == "hot":
                    r = hot_number(n) % HOT_RING
                    for j in range(HOT_TILES):
                        last = nc.tensor.matmul(t_ps[:, :], hot_split[r][0:HOT_P, j, :], one_hot[r][0:HOT_P, j, :],
                                                start=(j == 0), stop=(j == HOT_TILES - 1))
                else:
                    for q in range(2):
                        last = nc.tensor.matmul(t_ps[:, :], halves_sum[:, D - q * D:D - q * D + P],
                                                mover[:, mover_slot(2 * n + q), :], start=(q == 0), stop=(q == 1))
                last.then_inc(bank_filled, 1)

            def start_slot(s):
                c = SLOT_CHUNK[s]
                if c not in SLOT_CHUNK[:s]:
                    pe.wait_ge(w_high_ready, c + 1)
                    wait_low(pe, c)
                if s >= U_RING:
                    pe.wait_ge(prod_ready, s - U_RING + 1)

            def weights(s, first, cols):
                c, block = divmod(SLOT_BLOCK[s], CHUNK_TILES // GROUP_TILES)
                first += block * GROUP_TILES * P
                return (w[:, c % SPLIT_RING, first:first + cols] for w in (w_high, w_low))

            def multiply(t):
                m, i = TILE_LIST[t]
                s, k = divmod(place(t), SLOT_TILES)
                if i == 2 * m and m not in HOT_COUPLES:
                    wait_mover_low(pe, m)
                out = u_ps[:, SLOT_TILES * (s % U_RING) + k, :]
                high, low = weights(s, t % GROUP_TILES * P, P)
                nc.tensor.matmul(out, high, mover[:, mover_slot(i), :], start=True, stop=False)
                last = nc.tensor.matmul(out, low, mover[:, mover_slot(i), :], start=False, stop=True)
                if k == SLOT_TILES - 1:
                    last.then_inc(u_ready, 1)

            def multiply_unit(k):
                j, half = divmod(k, GROUP_SLOTS)
                wait_mover_low(pe, unit_couple(j))
                s = UNIT_SLOTS[k]
                high, low = weights(s, 0, UNIT_COLS)
                for side in range(SLOT_TILES):
                    bt = half * SLOT_TILES + side
                    out = u_ps[:, SLOT_TILES * (s % U_RING) + side, :]
                    values = mover[:, mover_slot(2 * LATER + j), bt * P:(bt + 1) * P]
                    nc.tensor.matmul(out, values, high, start=True, stop=False)
                    last = nc.tensor.matmul(out, values, low, start=False, stop=True)
                last.then_inc(u_ready, 1)

            def sum_group(g):
                pe.wait_ge(prod_ready, slots_through_group(g))
                for t in range(GROUP_TILES * g, GROUP_TILES * (g + 1)):
                    k, q, r = z_place(t)
                    if t % Z_TILES == 0 and k >= Z_RING:
                        pe.wait_ge(z_ready, k - Z_RING + 1)
                    final = r == z_rows[k, q] - 1
                    at = QUAD - 2 - 2 * r
                    last = nc.tensor.matmul(z_ps[QUAD * q:QUAD * (q + 1), k % Z_RING, :],
                                            selector[:, at:at + QUAD],
                                            prod[:, t // SLOT_TILES % PROD_RING, t % SLOT_TILES, :],
                                            start=(r == 0), stop=final)
                last.then_inc(sums_ready, 1)

            def layer1(out, z, n, start, stop):
                rows = P if z < Z_SUMMED else Z_TURNED_ROWS
                return nc.tensor.matmul(out, w1_sb[0:rows, z, n * P:(n + 1) * P], z_sb[0:rows, z, :],
                                        start=start, stop=stop)

            z_rows = {}
            for t in range(TILES):
                k, q, r = z_place(t)
                z_rows[k, q] = r + 1
            pe.wait_ge(identity_ready, 1)
            pe.wait_ge(selector_ready, 2)
            pe.wait_ge(halves_ready, 2)
            next_group = 0
            next_step = 0

            def fill_banks(place):
                nonlocal next_step
                while next_step < len(banked) and banked[next_step][0] <= place:
                    fill_bank(next_step)
                    next_step += 1

            def sum_groups(place):
                nonlocal next_group
                while next_group < GROUPS and place >= SLOT_TILES * (
                        slots_through_group(next_group) + SUM_LAG - GROUP_SLOTS
                        + GROUP_SLOTS * (next_group % Z_GROUPS == 0)):
                    sum_group(next_group)
                    next_group += 1

            for slot, (what, number) in enumerate(SLOT_LIST):
                fill_banks(SLOT_TILES * slot)
                start_slot(slot)
                if what == "unit":
                    multiply_unit(number)
                else:
                    for k in range(SLOT_TILES):
                        fill_banks(SLOT_TILES * slot + k)
                        multiply(SLOT_TILES * number + k)
                if slot == SLOTS - 1 or SLOT_LIST[slot + 1] != ("tiles", number + 1) or number % GROUP_SLOTS or what == "unit":
                    sum_groups(SLOT_TILES * (slot + 1))
            fill_banks(SLOT_TILES * SLOTS)

            wait_bank_left(pe, len(banked) - 1)
            for n in range(H1_TILES):
                if left_at[n]:
                    pe.wait_ge(prod_ready, left_at[n])
                layer1(h1_ps[n], Z_COUNT - 1, n, True, False)
                while next_group < GROUPS and slots_through_group(next_group) <= left_at[n] + 1:
                    sum_group(next_group)
                    next_group += 1
            assert next_group == GROUPS
            pe.wait_ge(z_ready, Z_SUMMED)
            for n in range(H1_TILES):
                layer1(h1_ps[n], Z_SUMMED - 1, n, False, True).then_inc(h1_summed, 1)
            pe.wait_ge(w2_loaded, 16)
            for k in range(H1_TILES):
                pe.wait_ge(h1_ready, k + 1)
                for n in range(H2_TILES):
                    last = nc.tensor.matmul(h2_ps[n], w2_sb[:, k, n * P:(n + 1) * P], h1_sb[:, k, :],
                                            start=(k == 0), stop=(k == H1_TILES - 1))
                    if k == H1_TILES - 1:
                        last.then_inc(h2_summed, 1)
            for k in range(H2_TILES):
                pe.wait_ge(h2_ready, k + 1)
                last = nc.tensor.matmul(y_ps, w3_sb[:, k:k + 1], h2_sb[:, k, :],
                                        start=(k == 0), stop=(k == H2_TILES - 1))
            last.then_inc(y_summed, 1)


def pair_index(i, j):
    return i * FIELDS - i * (i + 1) // 2 + j - i - 1


def kernel(**inputs):
    import concourse.bacc as bacc
    from concourse.bass_utils import run_bass_kernel_spmd

    small = [f for f in range(FIELDS) if inputs[f"tbl_{f}"].shape[0] == HOT_ROWS][:2 * len(HOT_COUPLES)]
    others = [f for f in range(FIELDS) if f not in small]
    order = [(small if q // 2 in HOT_COUPLES else others).pop(0) for q in range(FIELDS)]
    w = np.asarray(inputs["L0_rec_W"])
    w_sides = np.zeros((SLOT_TILES * SLOTS, 2, D, D), w.dtype)
    w1 = np.asarray(inputs["W_top1"])
    w1_rows = np.zeros((Z_COUNT, P, H1), w1.dtype)

    def pair_of(i, j):
        a, b = order[i], order[j]
        p = pair_index(min(a, b), max(a, b))
        return (w[p] if a < b else w[p].T), w1[p]

    for t, (m, i) in enumerate(TILE_LIST):
        k, q, r = z_place(t)
        for side in range(2):
            if i < 2 * m + side:
                at = GROUP_TILES * BLOCK_LIST.index(("tiles", t // GROUP_TILES)) + t % GROUP_TILES
                w_sides[at, side], w1_rows[k, QUAD * q + 2 * r + side] = pair_of(i, 2 * m + side)
    turned_rows = []
    for j in range(UNITS):
        first = GROUP_TILES * BLOCK_LIST.index(("unit", j))
        for o, field in enumerate(OCTET_FIELDS):
            w_sides[first + o // 2, o % 2], row = pair_of(2 * LATER + j, field)
            turned_rows.append(row)
    turned_rows += list(w1[-DENSE:])
    w1_rows[Z_SUMMED:, 0:Z_TURNED_ROWS] = np.reshape(turned_rows, (Z_TURNED, Z_TURNED_ROWS, H1))
    w_pairs = w_sides.reshape(CHUNKS, CHUNK_TILES, 2, D, D).transpose(0, 3, 1, 2, 4).reshape(CHUNKS, D, CHUNK_COLS)

    arrays = {
        "dense": np.asarray(inputs["dense_ctx"]),
        "ids": np.asarray(inputs["ids"])[:, order],
        "ids_t": np.asarray(inputs["ids"])[:, order].T,
        "w_pairs": w_pairs,
        "w1": w1_rows,
        "b1": np.asarray(inputs["b_top1"]).reshape(H1_TILES, P).T,
        "w2": np.asarray(inputs["W_top2"]),
        "b2": np.asarray(inputs["b_top2"]).reshape(H2_TILES, P).T,
        "w3": np.asarray(inputs["W_top3"]).reshape(H2_TILES, P).T,
    }
    for f in range(FIELDS):
        arrays[f"tbl_{f}"] = np.asarray(inputs[f"tbl_{f}"])
    arrays = {f"in_{name}": np.ascontiguousarray(a) for name, a in arrays.items()}

    nc = bacc.Bacc("TRN2", target_bir_lowering=False, num_devices=1)
    ap = {
        name[3:]: nc.dram_tensor(name, a.shape, mybir.dt.from_np(a.dtype), kind="ExternalInput").ap()
        for name, a in arrays.items()
    }
    y = nc.dram_tensor("out_y", (BATCH, 1), F32, kind="ExternalOutput").ap()
    tower(nc, ap["dense"], ap["ids"], ap["ids_t"], [ap[f"tbl_{f}"] for f in order], ap["w_pairs"],
          ap["w1"], ap["b1"], ap["w2"], ap["b2"], ap["w3"], y)
    result = run_bass_kernel_spmd(nc, [arrays], core_ids=[0])
    return result.results[0]["out_y"]
```
